# Optimizing a Trainium2 kernel written in Bass

```python
import numpy as np
import jax
import jax.numpy as jnp

def _softmax(x, axis=-1):
    return jax.nn.softmax(x, axis=axis)

def _gelu(x):
    return jax.nn.gelu(x, approximate=True)

def _silu(x):
    return jax.nn.silu(x)

def _sigmoid(x):
    return jax.nn.sigmoid(x)

def _layernorm(x, axis=-1, eps=1e-05):
    m = jnp.mean(x, axis=axis, keepdims=True)
    v = jnp.var(x, axis=axis, keepdims=True)
    return (x - m) / jnp.sqrt(v + eps)

def _scatter_add(tgt, idx, src, axis=0):
    return tgt.at[idx].add(src)

def _segment_sum(src, seg, n):
    return jax.ops.segment_sum(src, seg, n)
kernel_name = 'mk_sandwich_d1_jaxref_r4_3895c6'

def setup_inputs(seed: int=0):
    np.random.seed(seed)
    _w = jnp.asarray

    def _L0_attn_setup():
        import jax, jax.numpy as jnp
        import numpy as np
        import math
        B, S, D = (4, 512, 256)
        H = 16
        HD = D // H
        DL = 64
        LAMBDA_DECAY = 0.01
        key = jax.random.key(seed)
        ks = jax.random.split(key, 8)
        sc = lambda fan_in: 1.0 / math.sqrt(fan_in)
        return {'x': jax.random.normal(ks[0], (B, S, D), dtype=jnp.float32), 'W_q': jax.random.normal(ks[1], (D, D), dtype=jnp.float32) * sc(D), 'W_k': jax.random.normal(ks[2], (D, D), dtype=jnp.float32) * sc(D), 'W_v': jax.random.normal(ks[3], (D, D), dtype=jnp.float32) * sc(D), 'W_o': jax.random.normal(ks[4], (D, D), dtype=jnp.float32) * sc(D), 'W_down_kv': jax.random.normal(ks[5], (D, DL), dtype=jnp.float32) * sc(D), 'W_up_k': jax.random.normal(ks[6], (DL, D), dtype=jnp.float32) * sc(DL), 'W_up_v': jax.random.normal(ks[7], (DL, D), dtype=jnp.float32) * sc(DL)}
    _L0_attn_in = _L0_attn_setup()

    def _L0_ffn_setup():
        import jax, jax.numpy as jnp
        import numpy as np
        HIDDEN = 256
        N_ROUTED = 16
        N_SHARED = 2
        TOP_K = 2
        MID_R = HIDDEN // 4
        MID_S = HIDDEN // 2
        key = jax.random.key(seed)
        ks = jax.random.split(key, 8)
        s = 0.02
        return {'x': jax.random.normal(ks[0], (2, 256, HIDDEN), dtype=jnp.float32), 'router_w': jax.random.normal(ks[1], (HIDDEN, N_ROUTED), dtype=jnp.float32) * s, 'wg_r': jax.random.normal(ks[2], (N_ROUTED, HIDDEN, MID_R), dtype=jnp.float32) * s, 'wu_r': jax.random.normal(ks[3], (N_ROUTED, HIDDEN, MID_R), dtype=jnp.float32) * s, 'wd_r': jax.random.normal(ks[4], (N_ROUTED, MID_R, HIDDEN), dtype=jnp.float32) * s, 'wg_s': jax.random.normal(ks[5], (N_SHARED, HIDDEN, MID_S), dtype=jnp.float32) * s, 'wu_s': jax.random.normal(ks[6], (N_SHARED, HIDDEN, MID_S), dtype=jnp.float32) * s, 'wd_s': jax.random.normal(ks[7], (N_SHARED, MID_S, HIDDEN), dtype=jnp.float32) * s}
    _L0_ffn_in = _L0_ffn_setup()
    _d = {'L0_attn_x': _L0_attn_in['x'], 'L0_attn_W_q': _L0_attn_in['W_q'], 'L0_attn_W_k': _L0_attn_in['W_k'], 'L0_attn_W_v': _L0_attn_in['W_v'], 'L0_attn_W_o': _L0_attn_in['W_o'], 'L0_attn_W_down_kv': _L0_attn_in['W_down_kv'], 'L0_attn_W_up_k': _L0_attn_in['W_up_k'], 'L0_attn_W_up_v': _L0_attn_in['W_up_v'], 'L0_ffn_router_w': _L0_ffn_in['router_w'], 'L0_ffn_wg_r': _L0_ffn_in['wg_r'], 'L0_ffn_wu_r': _L0_ffn_in['wu_r'], 'L0_ffn_wd_r': _L0_ffn_in['wd_r'], 'L0_ffn_wg_s': _L0_ffn_in['wg_s'], 'L0_ffn_wu_s': _L0_ffn_in['wu_s'], 'L0_ffn_wd_s': _L0_ffn_in['wd_s']}
    _x0 = _d['L0_attn_x']
    _d['L0_attn_x'] = jax.random.normal(jax.random.fold_in(jax.random.key(seed), 1), (2, 2048, 256), dtype=_x0.dtype)
    del _x0
    return _d

def reference(L0_attn_x, L0_attn_W_q, L0_attn_W_k, L0_attn_W_v, L0_attn_W_o, L0_attn_W_down_kv, L0_attn_W_up_k, L0_attn_W_up_v, L0_ffn_router_w, L0_ffn_wg_r, L0_ffn_wu_r, L0_ffn_wd_r, L0_ffn_wg_s, L0_ffn_wu_s, L0_ffn_wd_s):

    def _L0_attn_ref(x, W_q, W_k, W_v, W_o, W_down_kv, W_up_k, W_up_v):
        import jax, jax.numpy as jnp
        import numpy as np
        import math
        B, S, D = (4, 512, 256)
        H = 16
        HD = D // H
        DL = 64
        LAMBDA_DECAY = 0.01
        b, s, d = x.shape
        q = x @ W_q
        k = x @ W_k
        v = x @ W_v
        latent_kv = (k + v) @ W_down_kv
        k_rec = (latent_kv @ W_up_k).reshape(b, s, H, HD).transpose(0, 2, 1, 3)
        v_rec = (latent_kv @ W_up_v).reshape(b, s, H, HD).transpose(0, 2, 1, 3)
        qh = q.reshape(b, s, H, HD).transpose(0, 2, 1, 3)
        scores = jnp.einsum('bhqd,bhkd->bhqk', qh, k_rec) / math.sqrt(d)
        t = jnp.arange(s, dtype=jnp.float32)
        decay = jnp.exp(-LAMBDA_DECAY * jnp.abs(t[:, None] - t[None, :]))
        scores = scores * decay[None, None, :, :]
        attn = jax.nn.softmax(scores, axis=-1)
        out = jnp.einsum('bhqk,bhkd->bhqd', attn, v_rec)
        out = out.transpose(0, 2, 1, 3).reshape(b, s, d)
        return out @ W_o

    def _L0_ffn_ref(x, router_w, wg_r, wu_r, wd_r, wg_s, wu_s, wd_s):
        import jax, jax.numpy as jnp
        import numpy as np
        HIDDEN = 256
        N_ROUTED = 16
        N_SHARED = 2
        TOP_K = 2
        MID_R = HIDDEN // 4
        MID_S = HIDDEN // 2
        orig_shape = x.shape
        flat = x.reshape(-1, orig_shape[-1])
        gs = jnp.einsum('td,ndm->tnm', flat, wg_s)
        us = jnp.einsum('td,ndm->tnm', flat, wu_s)
        out = jnp.einsum('tnm,nmd->td', jax.nn.silu(gs) * us, wd_s)
        logits = (flat @ router_w).astype(jnp.float32)
        probs = jax.nn.softmax(logits, axis=-1)
        weights, indices = jax.lax.top_k(probs, TOP_K)
        weights = weights / (weights.sum(axis=-1, keepdims=True) + 1e-09)
        weights = weights.astype(x.dtype)
        comb = jnp.sum(jax.nn.one_hot(indices, N_ROUTED, dtype=x.dtype) * weights[..., None], axis=1)
        g = jnp.einsum('td,edm->tem', flat, wg_r)
        u = jnp.einsum('td,edm->tem', flat, wu_r)
        h = jax.nn.silu(g) * u
        h = h * comb[:, :, None]
        out = out + jnp.einsum('tem,emd->td', h, wd_r)
        return out.reshape(orig_shape)
    x = L0_attn_x
    x = x + _layernorm(_L0_attn_ref(_layernorm(x, axis=-1), L0_attn_W_q, L0_attn_W_k, L0_attn_W_v, L0_attn_W_o, L0_attn_W_down_kv, L0_attn_W_up_k, L0_attn_W_up_v), axis=-1)
    x = x + _layernorm(_L0_ffn_ref(_layernorm(x, axis=-1), L0_ffn_router_w, L0_ffn_wg_r, L0_ffn_wu_r, L0_ffn_wd_r, L0_ffn_wg_s, L0_ffn_wu_s, L0_ffn_wd_s), axis=-1)
    return x

_drawn_inputs = setup_inputs


def setup_inputs(seed=0):
    import zlib

    import numpy as np

    out = dict(_drawn_inputs(seed))
    spreads = {}
    factors = {}
    for name, (base, spread) in spreads.items():
        noise = np.random.default_rng([zlib.crc32(name.encode()), seed]).standard_normal(out[name].shape)
        drawn = base * np.exp(spread * noise) if base else spread * noise
        out[name] = jnp.asarray(drawn.astype(out[name].dtype))
    for name, factor in factors.items():
        out[name] = (out[name] * factor).astype(out[name].dtype)
    return out
```

```python
import numpy as np
import concourse.bass as bass
from concourse import mybir
from contextlib import ExitStack

F32 = mybir.dt.float32
U32 = mybir.dt.uint32
BF16 = mybir.dt.bfloat16
ALU = mybir.AluOpType
ACT = mybir.ActivationFunctionType
AX = mybir.AxisListType

P = 128
B, S, D = 2, 2048, 256
T = B * S
H, HD = 16, 16
LAT = 64
DECAY = 0.01
KD = D // P
STRIP = 32
KT = S // P
CH = 512
QC = S // CH
CT = CH // P
NB = T // CH
NE, MR = 16, 64
NSH, MS = 2, 128
HT = (NSH * MS + NE * MR) // P
EPT = P // MR
LN_EPS = 1e-5
TOP_EPS = 1e-9
PRIME = 2


def emit(nc, io):
    ctx = ExitStack()
    with ctx:
        sb = lambda n, s, d=F32: ctx.enter_context(nc.sbuf_tensor(n, s, d))
        sem = lambda n: ctx.enter_context(nc.semaphore(n))

        ident = sb("ident", [P, P])
        small = sb("small", [P, 1152])
        xT = sb("xT", [P, KD, T])
        V_all = sb("V_all", [P, B * H, KT, HD])
        decay = sb("decay", [P, 2, S])
        w_qk = sb("w_qk", [P, 2, KD, D])
        w_unit = sb("w_unit", [P, 2, KD, P])
        stack = sb("stack", [P, 2, 4, S], BF16)
        part = sb("part", [P, 2, 2, 3, CH], BF16)
        work = sb("work", [P, 11520])
        ps = ctx.enter_context(nc.psum_tensor("ps", [P, 8, CH], F32))

        dram = lambda n, s: nc.dram_tensor(n, s, F32, kind="Internal").ap()
        attn_dram = dram("attn_dram", [T, D])
        parts_dram = nc.dram_tensor("parts_dram", [4, 3, B * H, HD, S], BF16, kind="Internal").ap()

        common = dict(nc=nc, io=io, sb=sb, sem=sem, ident=ident, xT=xT, V_all=V_all, decay=decay, small=small,
                      w_qk=w_qk, w_unit=w_unit, stack=stack, part=part, work=work, ps=ps,
                      attn_dram=attn_dram, parts_dram=parts_dram)
        prologue(**common)
        attention(**common)
        router(**common)
        experts(**common)


def carve(t, at, *shape):
    n = int(np.prod(shape))
    v = t[:, at:at + n]
    names = "abcd"[:len(shape)]
    if len(shape) > 1:
        v = v.rearrange(f"p ({' '.join(names)}) -> p {' '.join(names)}", **{k: s for k, s in zip(names[1:], shape[1:])})
    return v


def prologue(nc, io, sem, ident, xT, V_all, decay, small, w_qk, work, ps, **_):
    w_k = carve(work, 0, KD, D)
    w_v = carve(work, 512, KD, D)
    w_q = carve(work, 1024, KD, D)
    w_kv = carve(work, 1536, KD, D)
    w_kvT = carve(work, 2048, KD, D)
    w_dn = carve(work, 2560, KD, LAT)
    w_uk = carve(work, 2688, D)
    w_uv = carve(work, 2944, D)
    w_cT = carve(work, 3200, D)
    w_veff = carve(work, 3456, KD, D)
    xin = carve(work, 4096, 4, CT, D)
    xn = carve(work, 8192, 2, CT, D)
    bn = carve(small, 0, NB, CT, 6)
    mv = carve(small, 192, NB, CT, 2)
    ve = carve(small, 256, NB, CT)
    rs = carve(small, 288, NB, CT)
    mhalf = carve(small, 320, CT)

    ident_in, w_in, dec_in = sem("ident_in"), sem("w_in"), sem("dec_in")
    dec_ones = sem("dec_ones")
    x_in = [sem(f"x_in{i}") for i in range(4)]
    kv_sum, kvT_ps, kvT_sb = sem("kv_sum"), sem("kvT_ps"), sem("kvT_sb")
    cT_ps, cT_sb, eff_ps, eff_sb = sem("cT_ps"), sem("cT_sb"), sem("eff_ps"), sem("eff_sb")
    stats, aggr, var_eps, rstd, xn_ready = sem("stats"), sem("aggr"), sem("var_eps"), sem("rstd"), sem("xn_ready")
    half_set, xT_ps, xT_sb, v_ps, v_sb = sem("half_set"), sem("xT_ps"), sem("xT_sb"), sem("v_ps"), sem("v_sb")
    x_dram = io["L0_attn_x"].rearrange("b s d -> (b s) d").rearrange("(n j p) d -> n p j d", j=CT, p=P)
    rows = lambda w: w.rearrange("(k p) n -> p k n", p=P)

    with nc.Block() as block:
        @block.sync
        def _(sp):
            sp.dma_start(ident[:, :], io["c_ident"]).then_inc(ident_in, 16)
            for dst, name in ((w_k, "L0_attn_W_k"), (w_v, "L0_attn_W_v"), (w_dn, "L0_attn_W_down_kv"), (w_q, "L0_attn_W_q")):
                sp.dma_start(dst, rows(io[name])).then_inc(w_in, 16)
            sp.dma_start(w_uk[0:LAT], io["L0_attn_W_up_k"]).then_inc(w_in, 16)
            sp.dma_start(w_uv[0:LAT], io["L0_attn_W_up_v"]).then_inc(w_in, 16)
            for n in range(NB):
                if n >= 4:
                    sp.wait_ge(xn_ready, n - 3)
                sp.dma_start(xin[:, n % 4], x_dram[n]).then_inc(x_in[n % 4], 16)
            for r in range(P // STRIP):
                for sign in range(2):
                    sp.dma_start(decay[STRIP * r:STRIP * (r + 1), sign, :], io["c_decay"][sign]).then_inc(dec_in, 16)
            sp.wait_ge(w_in, 6 * 16)
            sp.wait_ge(dec_in, 8 * 16)

        @block.gpsimd
        def _(pool):
            nc.gpsimd.memset(mhalf, -0.5).then_inc(half_set, 1)
            pool.wait_ge(half_set, 1)
            for n in range(NB):
                pool.wait_ge(var_eps, n + 1)
                nc.gpsimd.tensor_tensor(rs[:, n], ve[:, n], mhalf, ALU.pow).then_inc(rstd, 1)

        @block.vector
        def _(dve):
            def normalise(n):
                dve.wait_ge(rstd, n + 1)
                if n >= 2:
                    dve.wait_ge(xT_ps, 2 * (n - 1))
                for j in range(CT):
                    i = nc.vector.tensor_scalar(xn[:, n % 2, j], xin[:, n % 4, j], mv[:, n, j, 0:1],
                                                rs[:, n, j:j + 1], ALU.subtract, ALU.mult)
                i.then_inc(xn_ready, 1)

            dve.wait_ge(w_in, 6 * 16)
            nc.vector.tensor_tensor(w_kv, w_k, w_v, ALU.add).then_inc(kv_sum, 1)
            nc.vector.tensor_copy(w_qk[:, 0], w_q)
            for n in range(NB):
                dve.wait_ge(x_in[n % 4], 16 * (n // 4 + 1))
                for j in range(CT):
                    i = nc.vector.bn_stats(bn[:, n, j], xin[:, n % 4, j])
                i.then_inc(stats, 1)
                dve.wait_ge(stats, n + 1)
                for j in range(CT):
                    i = nc.vector.bn_aggr(mv[:, n, j], bn[:, n, j])
                i.then_inc(aggr, 1)
                dve.wait_ge(aggr, n + 1)
                nc.vector.tensor_scalar(ve[:, n], mv[:, n, :, 1], LN_EPS, None, ALU.add).then_inc(var_eps, 1)
                if n == 1:
                    dve.wait_ge(eff_ps, 1)
                    nc.vector.tensor_copy(w_qk[:, 1], ps[:, 2, :].rearrange("p (k n) -> p k n", k=KD))
                    nc.vector.tensor_copy(w_veff, ps[:, 3, :].rearrange("p (k n) -> p k n", k=KD)).then_inc(eff_sb, 1)
                if n >= 1:
                    normalise(n - 1)
            normalise(NB - 1)

        @block.tensor
        def _(pe):
            pe.wait_ge(ident_in, 16)
            pe.wait_ge(kv_sum, 1)
            for k in range(KD):
                for i in range(KD):
                    m = nc.tensor.transpose(ps[:, 0, k * D + i * P:k * D + (i + 1) * P], w_kv[:, i, k * P:(k + 1) * P], ident[:, :])
            m.then_inc(kvT_ps, 1)
            pe.wait_ge(kvT_sb, 1)
            for k in range(KD):
                m = nc.tensor.matmul(ps[0:LAT, 1, 0:D], w_dn[:, k], w_kvT[:, k], start=k == 0, stop=k == KD - 1)
            m.then_inc(cT_ps, 1)
            pe.wait_ge(cT_sb, 1)
            for bank, up in ((2, w_uk), (3, w_uv)):
                for k in range(KD):
                    m = nc.tensor.matmul(ps[:, bank, k * D:(k + 1) * D], w_cT[0:LAT, k * P:(k + 1) * P], up[0:LAT], start=True, stop=True)
            m.then_inc(eff_ps, 1)
            for n in range(NB):
                pe.wait_ge(xn_ready, n + 1)
                if n >= 1:
                    pe.wait_ge(xT_sb, 2 * n)
                for k in range(KD):
                    for j in range(CT):
                        m = nc.tensor.transpose(ps[:, 4 + k, j * P:(j + 1) * P], xn[:, n % 2, j, k * P:(k + 1) * P], ident[:, :])
                    m.then_inc(xT_ps, 1)
                if n == 0:
                    pe.wait_ge(eff_sb, 1)
                pe.wait_ge(xT_sb, 2 * n + 2)
                for j in range(CT):
                    if j % 2 == 0 and n >= 1:
                        pe.wait_ge(v_sb, 2 * (n - 1) + j // 2 + 1)
                    for k in range(KD):
                        at = (n * CT + j) * P
                        m = nc.tensor.matmul(ps[:, 6 + j // 2, (j % 2) * D:(j % 2 + 1) * D], xT[:, k, at:at + P],
                                             w_veff[:, k], start=k == 0, stop=k == KD - 1)
                    if j % 2:
                        m.then_inc(v_ps, 1)

        @block.scalar
        def _(act):
            act.wait_ge(kvT_ps, 1)
            nc.scalar.copy(w_kvT, ps[:, 0, :].rearrange("p (k n) -> p k n", k=KD)).then_inc(kvT_sb, 1)
            act.wait_ge(cT_ps, 1)
            nc.scalar.copy(w_cT[0:LAT], ps[0:LAT, 1, 0:D]).then_inc(cT_sb, 1)
            for n in range(NB):
                for k in range(KD):
                    act.wait_ge(xT_ps, 2 * n + k + 1)
                    nc.scalar.copy(xT[:, k, n * CH:(n + 1) * CH], ps[:, 4 + k, :]).then_inc(xT_sb, 1)
                for i in range(2):
                    act.wait_ge(v_ps, 2 * n + i + 1)
                    b, kt = divmod(n * CT + 2 * i, KT)
                    for j in range(2):
                        v = nc.scalar.copy(V_all[:, b * H:(b + 1) * H, kt + j], ps[:, 6 + i, j * D:(j + 1) * D].rearrange("p (h d) -> p h d", h=H))
                    v.then_inc(v_sb, 1)


def attention(nc, io, sb, sem, ident, xT, V_all, decay, small, w_qk, w_unit, stack, part, work, ps, attn_dram, parts_dram, **_):
    probs = carve(work, 0, 2, S)
    diag_s = carve(work, 4096, S)
    Vg = carve(work, 6144, 2, KT, STRIP)
    O_sb = carve(work, 7168, CH)
    att = carve(work, 7680, KT, 2 * HD)
    split = carve(work, 8192, 2, CH)
    dmask = carve(small, 0, P)
    dmaskT = carve(small, 128, P)
    rden = carve(small, 256, CT, QC)
    mpart = carve(small, 288, KT, QC)
    mneg = carve(small, 352, P)
    mrow = carve(small, 480, P)
    mleft = carve(small, 608, P)
    mrow3 = carve(small, 736, 3 * P // 2).bitcast(BF16).rearrange("p (i q) -> p i q", i=3)
    QL, QU, KL, KU = range(4)
    ACC = 6

    names = ("vg w proj_ps proj_free prep_link prep_sb sc_ps exp_done pv_done o_sb oT_ps rden_sb att_sb d_ps d_sb "
             "mx_ps mx_mul mx_red mx_all mx_neg mxT_ps mx_link mx_part mx_rows z_ps z_add").split()
    s_ = {n: sem("a_" + n) for n in names}
    s_.update(att_out=sem("a_att_out"), stk0=sem("a_stk0"), stk1=sem("a_stk1"), out0=sem("a_out0"), out1=sem("a_out1"))
    cst_in, vg_set, stack_set, mneg_set = sem("cst_in"), sem("vg_set"), sem("stack_set"), sem("mneg_set")
    wait = lambda eng, name, v: eng.wait_ge(s_[name], v + PRIME)
    prime = lambda eng, *ns: [eng.sem_inc(s_[n], PRIME) for n in ns]

    NSTEP = KT + 1
    NPAIR = B * H // 2
    PPU = P // HD // 2
    ROWS = 6 * HD
    chunk = lambda c: slice(c * CH, (c + 1) * CH)

    def cut(lo, hi):
        while lo < hi:
            end = min(hi, (lo // CH + 1) * CH)
            yield lo, end
            lo = end

    def score_pieces(kt):
        for lo, hi in cut(0, kt * P):
            yield lo, hi - lo, lo, QU, KU
        for lo, hi in cut(kt * P, S - P):
            yield lo, hi - lo, lo + P, QL, KL

    def product_pieces(kt):
        first, rest = [], []
        for c in range(QC):
            lo, hi = c * CH, (c + 1) * CH
            if not lo <= kt * P < hi:
                first.append((c, 0, lo if hi <= kt * P else lo - P, CH))
                continue
            own = [(c, 0, lo, kt * P - lo), (c, kt * P + P - lo, kt * P, hi - kt * P - P)]
            own = [x for x in own if x[3]]
            first.append(own[0])
            rest += own[1:]
        return first + rest

    def pairs(eng, pair):
        pair(0, True, True, False)
        with eng.Fori(1, NPAIR - PPU) as it:
            pair(it, True, False, False)
        with eng.Fori(NPAIR - PPU, NPAIR - 1) as it:
            pair(it, False, False, False)
        pair(NPAIR - 1, False, False, True)

    with nc.Block() as block:
        @block.sync
        def _(sp):
            sp.dma_start(dmask, io["c_diag"][0]).then_inc(cst_in, 16)
            sp.dma_start(dmaskT, io["c_diag"][1]).then_inc(cst_in, 16)

            def load_stack(m, par):
                for kind in range(4):
                    for row, pt in enumerate((0, 0, 0, 1, 1, 2) if kind in (QL, QU) else (0, 1, 2, 0, 1, 0)):
                        src = parts_dram[kind, pt, bass.ds(m, 1)].rearrange("o d s -> (o d) s")
                        sp.dma_start(stack[row * HD:(row + 1) * HD, par, kind, :], src).then_inc(s_[f"stk{par}"], 16)

            def store_parts(unit, c, which, k):
                wait(sp, "prep_sb", k + 1)
                for a in range(2):
                    kind = 2 * which + a
                    dst = parts_dram[kind].rearrange("i h d s -> i (h d) s")
                    dst = dst[:, bass.ds(unit * P, P), bass.ds(c * CH, CH)].rearrange("i r s -> r i s")
                    sp.dma_start(dst, part[:, which, a]).then_inc(s_[f"out{which}"], 16)

            def store_att(it):
                wait(sp, "att_sb", 2 * it + 2)
                dst = attn_dram.rearrange("(b t p) (u d) -> b u p t d", b=B, p=P, d=2 * HD)
                sp.dma_start(dst[bass.ds(it // (H // 2), 1), bass.ds(it % (H // 2), 1)].rearrange("b u p t d -> p (b u t) d"), att).then_inc(s_["att_out"], 16)

            def shift_rows(m, par):
                wait(sp, "mx_link", 4 * (m + 1))
                for q in (QL, QU):
                    for i in range(3):
                        dst = stack[ROWS + i:ROWS + i + 1, par, q, :].rearrange("a (t p) -> a t p", p=P)
                        sp.dma_start(dst, mrow3[0:KT, i, :]).then_inc(s_["mx_rows"], 16)

            for c in range(QC):
                for which in range(2):
                    store_parts(0, c, which, 2 * c + which)
            for which in range(2):
                wait(sp, f"out{which}", 32 * QC)
            sp.wait_ge(stack_set, 4)
            load_stack(0, 0)
            shift_rows(0, 0)

            def pair(it, prep, first, last):
                for par in range(2):
                    n = it * 2 + par
                    end = last and par
                    if not end:
                        wait(sp, "sc_ps", n * KT)
                        if not first:
                            for which in range(2):
                                wait(sp, f"out{which}", ((it + par) // PPU + 1) * (32 * QC))
                        load_stack(n + 1, 1 - par)
                    if par == 0 and not first:
                        store_att(it - 1)
                    if par == 0 and prep:
                        for which in range(2):
                            store_parts(it // PPU + 1, it % PPU, which, 2 * QC + 2 * it + which)
                    if not end:
                        shift_rows(n + 1, 1 - par)
            pairs(sp, pair)
            store_att(NPAIR - 1)
            wait(sp, "att_out", 16 * NPAIR)

        @block.gpsimd
        def _(pool):
            prime(pool, "vg", "w", "att_out", "stk0", "stk1", "out0", "out1", "mx_rows")

            def values(m, par):
                nc.gpsimd.tensor_copy(Vg[:, par, :, 0:HD], V_all[:, bass.ds(m, 1)].rearrange("p o k d -> p (o k) d")).then_inc(s_["vg"], 1)

            def weights(half):
                nc.gpsimd.tensor_copy(w_unit[:, :, :, :], w_qk[:, :, :, bass.ds(half * P, P)]).then_inc(s_["w"], 1)

            weights(0)
            nc.gpsimd.memset(Vg, 0.0).then_inc(vg_set, 1)
            pool.wait_ge(vg_set, 1)
            nc.gpsimd.memset(Vg.rearrange("p a k c -> p (a k) c")[:, :, HD:HD + 1], 1.0).then_inc(vg_set, 1)
            pool.wait_ge(vg_set, 2)
            values(0, 0)

            def pair(it, prep, first, last):
                for par in range(2):
                    n = it * 2 + par
                    if par == 0 and prep:
                        wait(pool, "proj_ps", 2 * QC + 2 * it)
                        weights((it // PPU + 1) % KD)
                    if not (last and par):
                        wait(pool, "pv_done", n * NSTEP)
                        values(n + 1, 1 - par)
            pairs(pool, pair)

        @block.vector
        def _(dve):
            prime(dve, *"proj_free prep_link prep_sb o_sb rden_sb att_sb d_sb mx_mul mx_red mx_all mx_neg mx_link mx_part z_add".split())

            def prepare(c, which, k, bank):
                at = slice(c * CH, (c + 1) * CH) if isinstance(c, int) else bass.ds(c * CH, CH)
                pt = part[:, which]
                wait(dve, "prep_sb", k)
                wait(dve, "proj_ps", k + 1)
                wait(dve, f"out{which}", k // 2 * 32)
                nc.vector.tensor_tensor(split[:, 0], ps[:, bank], decay[:, which, at], ALU.mult)
                nc.vector.tensor_tensor(split[:, 1], ps[:, bank], decay[:, 1 - which, at], ALU.mult).then_inc(s_["proj_free"], 1)
                wait(dve, "proj_free", k + 1)
                nc.vector.tensor_copy(pt[:, :, 0], split).then_inc(s_["prep_link"], 1)
                wait(dve, "prep_link", 3 * k + 1)
                nc.vector.tensor_tensor(split, split, pt[:, :, 0], ALU.subtract).then_inc(s_["prep_link"], 1)
                wait(dve, "prep_link", 3 * k + 2)
                nc.vector.tensor_copy(pt[:, :, 1], split).then_inc(s_["prep_link"], 1)
                wait(dve, "prep_link", 3 * k + 3)
                nc.vector.tensor_tensor(pt[:, :, 2], split, pt[:, :, 1], ALU.subtract).then_inc(s_["prep_sb"], 1)

            def normalise(m, par, first_pair):
                wait(dve, "pv_done", (m + 1) * NSTEP)
                nc.vector.tensor_copy(O_sb, ps[:, ACC + par]).then_inc(s_["o_sb"], 1)
                wait(dve, "oT_ps", m + 1)
                oT = ps[:, ACC + par].rearrange("p (j c d) -> p j c d", j=CT, c=QC)
                nc.vector.reciprocal(rden, oT[:, :, :, HD]).then_inc(s_["rden_sb"], 1)
                wait(dve, "rden_sb", m + 1)
                if par == 0:
                    wait(dve, "att_out", m // 2 * 16)
                dst = att[:, :, par * HD:(par + 1) * HD].rearrange("p (c j) d -> p j c d", c=QC)
                nc.vector.tensor_tensor(dst, oT[:, :, :, 0:HD], rden.unsqueeze(3).to_broadcast([P, CT, QC, HD]),
                                        ALU.mult).then_inc(s_["att_sb"], 1)

            def diagonals(m, bank):
                wait(dve, "exp_done", (m - 1) * (2 * NSTEP) + 2 if not isinstance(m, int) or m else 0)
                for c in range(QC):
                    wait(dve, "d_ps", m * QC + c + 1)
                    nc.vector.tensor_tensor(diag_s[:, chunk(c)].rearrange("p (j m) -> p j m", m=P),
                                            ps[:, bank].rearrange("p (j m) -> p j m", m=P),
                                            dmask.unsqueeze(1).to_broadcast([P, CT, P]), ALU.mult).then_inc(s_["d_sb"], 1)

            def maxima(m, bank):
                for t in range(KT):
                    for kc in range(QC):
                        wait(dve, "mx_ps", m * (KT * QC) + t * QC + kc + 1)
                        if kc == t // CT:
                            blk = ps[:, bank, t % CT * P:(t % CT + 1) * P]
                            nc.vector.tensor_tensor(blk, blk, dmaskT, ALU.mult).then_inc(s_["mx_mul"], 1)
                            wait(dve, "mx_mul", m * KT + t + 1)
                        nc.vector.tensor_reduce(mpart[:, t, kc:kc + 1], ps[:, bank], AX.X, ALU.max).then_inc(s_["mx_red"], 1)
                wait(dve, "mx_red", (m + 1) * (KT * QC))
                nc.vector.tensor_reduce(mneg[:, 0:KT], mpart, AX.X, ALU.max).then_inc(s_["mx_all"], 1)
                wait(dve, "mx_all", m + 1)
                nc.vector.tensor_scalar(mneg[:, 0:KT], mneg[:, 0:KT], -1.0, None, ALU.mult).then_inc(s_["mx_neg"], 1)
                wait(dve, "mxT_ps", m + 1)
                if not isinstance(m, int) or m:
                    wait(dve, "mx_rows", m * (6 * 16))
                nc.vector.tensor_copy(mleft[0:KT], ps[0:KT, bank, 0:P]).then_inc(s_["mx_link"], 1)
                wait(dve, "mx_link", 4 * m + 1)
                nc.vector.tensor_copy(mrow3[0:KT, 0], mleft[0:KT])
                nc.vector.tensor_copy(mrow[0:KT], mleft[0:KT]).then_inc(s_["mx_link"], 1)
                wait(dve, "mx_link", 4 * m + 2)
                nc.vector.tensor_tensor(mleft[0:KT], mrow[0:KT], mrow3[0:KT, 0], ALU.subtract).then_inc(s_["mx_link"], 1)
                wait(dve, "mx_link", 4 * m + 3)
                nc.vector.tensor_copy(mrow3[0:KT, 1], mleft[0:KT]).then_inc(s_["mx_part"], 1)
                wait(dve, "mx_part", m + 1)
                nc.vector.tensor_tensor(mrow3[0:KT, 2], mleft[0:KT], mrow3[0:KT, 1], ALU.subtract).then_inc(s_["mx_link"], 1)
                for c in range(QC):
                    wait(dve, "z_ps", m * QC + c + 1)
                    nc.vector.tensor_tensor(diag_s[:, chunk(c)], diag_s[:, chunk(c)], ps[:, bank], ALU.add).then_inc(s_["z_add"], 1)

            for par in range(2):
                nc.vector.memset(stack[ROWS:P, par, QL:QU + 1, :], 0.0).then_inc(stack_set, 1)
                nc.vector.memset(stack[ROWS:P, par, KL:KU + 1, :], 1.0).then_inc(stack_set, 1)
            nc.vector.memset(mneg, 0.0).then_inc(mneg_set, 1)
            dve.wait_ge(mneg_set, 1)
            dve.wait_ge(cst_in, 2 * 16)
            for c in range(QC):
                for which in range(2):
                    prepare(c, which, 2 * c + which, ACC + 1)
            diagonals(0, ACC + 1)
            maxima(0, ACC + 1)

            def pair(it, prep, first, last):
                for par in range(2):
                    n = it * 2 + par
                    idle = ACC + 1 - par
                    if not (first and par == 0):
                        normalise(n - 1, 1 - par, first)
                    if par == 0 and prep:
                        for which in range(2):
                            prepare(it % PPU, which, 2 * QC + 2 * it + which, idle)
                    if not (last and par):
                        diagonals(n + 1, idle)
                        maxima(n + 1, idle)
            pairs(dve, pair)
            normalise(B * H - 1, 1, False)

        @block.tensor
        def _(pe):
            prime(pe, *"proj_ps sc_ps pv_done oT_ps d_ps mx_ps mxT_ps z_ps".split())

            def project(at, which, bank):
                for k in range(KD):
                    m = nc.tensor.matmul(ps[:, bank], w_unit[:, which, k], xT[:, k, at:at + CH] if isinstance(at, int) else xT[:, k, bass.ds(at, CH)],
                                         start=k == 0, stop=k == KD - 1)
                m.then_inc(s_["proj_ps"], 1)

            def scores(par, n, s):
                wait(pe, "exp_done", n * (2 * NSTEP) + (2 * s - 1 if s > 1 else 0))
                for col, w, q0, q, k in score_pieces(s - 1):
                    bank = (QC * (s - 1) + col // CH) % ACC
                    m = nc.tensor.matmul(ps[:, bank, col % CH:col % CH + w], stack[0:ROWS + 3, par, k, (s - 1) * P:s * P],
                                         stack[0:ROWS + 3, par, q, q0:q0 + w], start=True, stop=True)
                m.then_inc(s_["sc_ps"], 1)

            def products(par, n, s):
                wait(pe, "exp_done", n * (2 * NSTEP) + 2 * s + 2)
                if s:
                    todo = [(s - 1, x) for x in product_pieces(s - 1)]
                else:
                    todo = [(c * CT + j, (c, j * P, c * CH + j * P, P)) for j in range(CT) for c in range(QC)]
                for i, (kt, (c, acol, pcol, w)) in enumerate(todo):
                    m = nc.tensor.matmul(ps[STRIP * c:STRIP * (c + 1), ACC + par, acol:acol + w], Vg[:, par, kt],
                                         probs[:, (s + par) % 2, pcol:pcol + w], start=s == 0 and i < QC,
                                         stop=s == NSTEP - 1 and i >= len(todo) - QC, skip_group_check=True)
                m.then_inc(s_["pv_done"], 1)

            def transposes(m, par):
                wait(pe, "o_sb", m + 1)
                for j in range(CT):
                    i = nc.tensor.transpose(ps[:, ACC + par, j * P:(j + 1) * P], O_sb[:, j * P:(j + 1) * P], ident[:, :])
                i.then_inc(s_["oT_ps"], 1)

            def diagonal(m, par, c, bank):
                for j in range(CT):
                    at = (c * CT + j) * P
                    i = nc.tensor.matmul(ps[:, bank, j * P:(j + 1) * P], stack[0:ROWS, par, KL, at:at + P],
                                         stack[0:ROWS, par, QL, at:at + P], start=True, stop=True)
                i.then_inc(s_["d_ps"], 1)

            def maxima(m, par, bank):
                for t in range(KT):
                    for kc in range(QC):
                        if t or kc:
                            wait(pe, "mx_red", m * (KT * QC) + t * QC + kc)
                        lo, hi = kc * CH, (kc + 1) * CH
                        mid = min(max((t + 1) * P, lo), hi)
                        for a, z, q, k in ((lo, mid, QL, KL), (mid, hi, QU, KU)):
                            if a < z:
                                i = nc.tensor.matmul(ps[:, bank, a - lo:z - lo], stack[0:ROWS, par, q, t * P:(t + 1) * P],
                                                     stack[0:ROWS, par, k, a:z], start=True, stop=True)
                        i.then_inc(s_["mx_ps"], 1)
                wait(pe, "mx_neg", m + 1)
                nc.tensor.transpose(ps[:, bank, 0:P], mneg, ident[:, :]).then_inc(s_["mxT_ps"], 1)
                wait(pe, "mx_link", 4 * m + 1)
                wait(pe, "mx_rows", (m + 1) * (6 * 16))
                for c in range(QC):
                    if c:
                        wait(pe, "z_add", m * QC + c)
                    nc.tensor.matmul(ps[:, bank], stack[ROWS:ROWS + 3, par, KL, 0:P], stack[ROWS:ROWS + 3, par, QL, chunk(c)],
                                     start=True, stop=True).then_inc(s_["z_ps"], 1)

            wait(pe, "w", 1)
            for k in range(2 * QC):
                if k:
                    wait(pe, "proj_free", k)
                project(k // 2 * CH, k % 2, ACC + 1)
            wait(pe, "proj_free", 2 * QC)
            wait(pe, "stk0", 24 * 16)
            for c in range(QC):
                if c:
                    wait(pe, "d_sb", c)
                diagonal(0, 0, c, ACC + 1)
            wait(pe, "d_sb", QC)
            pe.wait_ge(stack_set, 4)
            maxima(0, 0, ACC + 1)

            def pair(it, prep, first, last):
                for par in range(2):
                    n = it * 2 + par
                    idle = ACC + 1 - par
                    end = last and par
                    wait(pe, "vg", n + 1)
                    for s in range(1, NSTEP):
                        scores(par, n, s)
                        products(par, n, s - 1)
                        if s == 2 and not (first and par == 0):
                            transposes(n - 1, 1 - par)
                        if par == 0 and prep:
                            at = ((it // PPU + 1) // KD) * S + (it % PPU) * CH
                            if s == 4:
                                wait(pe, "w", it + 2)
                                if not first:
                                    wait(pe, "att_sb", n)
                                project(at, 0, idle)
                            if s == 8:
                                wait(pe, "proj_free", 2 * QC + 2 * it + 1)
                                project(at, 1, idle)
                        if s >= NSTEP - QC and not end:
                            c = s - (NSTEP - QC)
                            if c:
                                wait(pe, "d_sb", (n + 1) * QC + c)
                            else:
                                wait(pe, "stk" + str(1 - par), (it + 1 + par) * 384)
                                if par == 0 and prep:
                                    wait(pe, "proj_free", 2 * QC + 2 * it + 2)
                                elif not (first and par == 0):
                                    wait(pe, "att_sb", n)
                            diagonal(n + 1, 1 - par, c, idle)
                    products(par, n, NSTEP - 1)
                    if not end:
                        wait(pe, "d_sb", (n + 2) * QC)
                        maxima(n + 1, 1 - par, idle)
            pairs(pe, pair)
            transposes(B * H - 1, 1)

        @block.scalar
        def _(act):
            prime(act, "exp_done")

            def pair(it, prep, first, last):
                for par in range(2):
                    n = it * 2 + par
                    for s in range(NSTEP):
                        for p in range(2):
                            lo, hi = p * 2 * CH, min((p + 1) * 2 * CH, S - P if s else S)
                            if s:
                                if p == 0:
                                    wait(act, "sc_ps", n * KT + s)
                                bank = (QC * (s - 1) + 2 * p) % ACC
                                src = ps[:, bank:bank + 2].rearrange("p a b -> p (a b)")[:, 0:hi - lo]
                            else:
                                wait(act, "z_add", n * QC + 2 * p + 2)
                                src = diag_s[:, lo:hi]
                            if p == 0:
                                wait(act, "pv_done", n * NSTEP + s - 1)
                            nc.scalar.activation(probs[:, (s + par) % 2, lo:hi], src, ACT.Exp, scale=1.0 / D ** 0.5).then_inc(s_["exp_done"], 1)
            pairs(act, pair)


def router(nc, io, sem, ident, xT, V_all, decay, small, w_qk, stack, work, ps, attn_dram, **_):
    x1 = V_all[:, :, :, :].rearrange("p h k d -> p h (k d)")
    combT = decay[0:NE].rearrange("p a t -> p (a t)")
    at_in = carve(work, 0, 2, CT, D)
    x_in = carve(work, 2048, 2, CT, D)
    aT = carve(work, 4096, KD, CH)
    yn = carve(work, 5120, CT, D)
    xn = carve(work, 6144, CT, D)
    x1b = carve(work, 7168, CT, D)
    x2s = carve(work, 8192, KD, CH)
    w_r = carve(work, 9216, KD, NE)
    bn = carve(small, 0, CT, 6)
    mv = carve(small, 32, CT, 2)
    ve = carve(small, 48, CT)
    rs = carve(small, 56, CT)
    mhalf = carve(small, 64, CT)
    lmax = carve(small, 72, CT)
    lsub = carve(small, 80, CT, NE)
    ex = carve(small, 144, CT, NE)
    zsum = carve(small, 208, CT)
    top = carve(small, 216, CT, 8)
    den = carve(small, 248, CT)
    wts = carve(small, 256, CT, 2)
    idxf = carve(small, 272, CT, 8)
    first = carve(small, 304, CT, NE)
    comb = carve(small, 368, CT, NE)
    iota = carve(small, 432, NE)
    idx = carve(small, 448, CT, 8).bitcast(U32)

    a_in, xr_in, c_in = [sem(f"a_in{i}") for i in range(2)], [sem(f"xr_in{i}") for i in range(2)], sem("c_in")
    aT_ps, aT_sb, y_ps, dve_c, ve1, rs1, x1_sb, ve2, rs2, xn_sb = (sem(n) for n in (
        "aT_ps", "aT_sb", "y_ps", "dve_c", "ve1", "rs1", "x1_sb", "ve2", "rs2", "xn_sb"))
    x2_ps, x2_sb, x2_cp, lg_ps, lsub_sb, ex_sb, comb_sb, cT_ps2, cT_sb2, half2, x1_cp = (sem(n) for n in (
        "x2_ps", "x2_sb", "x2_cp", "lg_ps", "lsub_sb", "ex_sb", "comb_sb", "cT_ps2", "cT_sb2", "half2", "x1_cp"))
    ffn_in = sem("ffn_in")
    a_dram = attn_dram.rearrange("(n j p) d -> p n j d", j=CT, p=P)
    x_dram = io["L0_attn_x"].rearrange("b s d -> (b s) d").rearrange("(n j p) d -> p n j d", j=CT, p=P)
    w_up, w_dn = ffn_weights(stack)
    w_o = w_qk[:, 0]

    def loop(eng, body):
        with eng.Fori(0, NB // 2) as i:
            for par in range(2):
                body(i * 2 + par, par, i)

    with nc.Block() as block:
        @block.sync
        def _(sp):
            sp.dma_start(w_o, io["L0_attn_W_o"].rearrange("(k p) n -> p k n", p=P)).then_inc(c_in, 16)
            sp.dma_start(w_r, io["L0_ffn_router_w"].rearrange("(k p) n -> p k n", p=P)).then_inc(c_in, 16)
            sp.dma_start(iota, io["c_iota"]).then_inc(c_in, 16)
            sp.dma_start(at_in[:, 0], a_dram[:, 0]).then_inc(a_in[0], 16)
            sp.dma_start(x_in[:, 0], x_dram[:, 0]).then_inc(xr_in[0], 16)
            sp.dma_start(at_in[:, 1], a_dram[:, 1]).then_inc(a_in[1], 16)
            sp.dma_start(x_in[:, 1], x_dram[:, 1]).then_inc(xr_in[1], 16)
            rows = lambda w: w.rearrange("(k p) m -> p k m", p=P)
            for i, (r, s) in enumerate((("L0_ffn_wg_r", "L0_ffn_wg_s"), ("L0_ffn_wu_r", "L0_ffn_wu_s"))):
                for e in range(NSH):
                    sp.dma_start(w_up[:, i, :, e], rows(io[s][e])).then_inc(ffn_in, 16)
                for e in range(NE):
                    dst = w_up[:, i, :, NSH + e // EPT, (e % EPT) * MR:(e % EPT + 1) * MR]
                    sp.dma_start(dst, rows(io[r][e])).then_inc(ffn_in, 16)
            sp.dma_start(w_dn[:, 0:NSH], io["L0_ffn_wd_s"].rearrange("e m d -> m e d")).then_inc(ffn_in, 16)
            sp.dma_start(w_dn[:, NSH:], io["L0_ffn_wd_r"].rearrange("(h e) m d -> (e m) h d", e=EPT)).then_inc(ffn_in, 16)
            with sp.Fori(0, NB // 2 - 1) as i:
                for par in range(2):
                    n = i * 2 + par
                    sp.wait_ge(aT_ps, n + 1)
                    sp.dma_start(at_in[:, par], a_dram[:, bass.ds(n + 2, 1)].rearrange("p o j d -> p (o j) d")).then_inc(a_in[par], 16)
                    sp.wait_ge(x1_sb, n + 1)
                    sp.dma_start(x_in[:, par], x_dram[:, bass.ds(n + 2, 1)].rearrange("p o j d -> p (o j) d")).then_inc(xr_in[par], 16)
            sp.wait_ge(ffn_in, 16 * (2 * (NSH + NE) + 2))

        @block.gpsimd
        def _(pool):
            pool.sem_inc(x2_cp, PRIME)
            nc.gpsimd.memset(mhalf, -0.5).then_inc(half2, 1)
            pool.wait_ge(half2, 1)

            def body(n, par, i):
                pool.wait_ge(ve1, n + 1)
                nc.gpsimd.tensor_tensor(rs, ve, mhalf, ALU.pow).then_inc(rs1, 1)
                pool.wait_ge(ve2, n + 1)
                nc.gpsimd.tensor_tensor(rs, ve, mhalf, ALU.pow).then_inc(rs2, 1)
                pool.wait_ge(x2_sb, 2 * n + 2)
                nc.gpsimd.tensor_copy(xT[:, :, bass.ds(n * CH, CH)], x2s).then_inc(x2_cp, 1)
            loop(pool, body)

        @block.vector
        def _(dve):
            def body(n, par, i):
                count = [0]

                def link(ins):
                    count[0] += 1
                    ins.then_inc(dve_c, 1)
                    dve.wait_ge(dve_c, n * LINKS + count[0])

                def stats(src):
                    for j in range(CT):
                        i_ = nc.vector.bn_stats(bn[:, j], src(j))
                    link(i_)
                    nc.vector.memset(ve, LN_EPS)
                    for j in range(CT):
                        i_ = nc.vector.bn_aggr(mv[:, j], bn[:, j])
                    link(i_)
                    return nc.vector.tensor_tensor(ve, ve, mv[:, :, 1], ALU.add)

                y = lambda j: ps[:, 2 + j // 2, (j % 2) * D:(j % 2 + 1) * D]
                dve.wait_ge(y_ps, n + 1 + PRIME)
                stats(y).then_inc(ve1, 1)
                dve.wait_ge(rs1, n + 1)
                for j in range(CT):
                    i_ = nc.vector.tensor_scalar(yn[:, j], y(j), mv[:, j, 0:1], rs[:, j:j + 1], ALU.subtract, ALU.mult)
                link(i_)
                dve.wait_ge(xr_in[par], i * 16 + 16)
                nc.vector.tensor_tensor(x1b, yn, x_in[:, par], ALU.add).then_inc(x1_sb, 1)
                dve.wait_ge(x1_sb, n + 1)
                nc.vector.tensor_copy(x1[:, bass.ds(n * CT, CT), :], x1b)
                stats(lambda j: x1b[:, j]).then_inc(ve2, 1)
                dve.wait_ge(rs2, n + 1)
                for j in range(CT):
                    i_ = nc.vector.tensor_scalar(xn[:, j], x1b[:, j], mv[:, j, 0:1], rs[:, j:j + 1], ALU.subtract, ALU.mult)
                i_.then_inc(xn_sb, 1)
                dve.wait_ge(lg_ps, n + 1 + PRIME)
                lg = ps[:, 6, 0:CT * NE].rearrange("p (j e) -> p j e", j=CT)
                bc = lambda v, w: v.unsqueeze(2).to_broadcast([P, CT, w])
                link(nc.vector.tensor_reduce(lmax, lg, AX.X, ALU.max))
                nc.vector.tensor_tensor(lsub, lg, bc(lmax, NE), ALU.subtract).then_inc(lsub_sb, 1)
                dve.wait_ge(ex_sb, n + 1)
                nc.vector.tensor_reduce(zsum, ex, AX.X, ALU.add)
                for j in range(CT):
                    i_ = nc.vector.max(top[:, j], ex[:, j])
                link(i_)
                nc.vector.scalar_tensor_tensor(den, zsum, TOP_EPS, top[:, :, 0], ALU.mult, ALU.add)
                for j in range(CT):
                    i_ = nc.vector.max_index(idx[:, j], top[:, j], ex[:, j])
                link(i_)
                nc.vector.tensor_copy(idxf, idx)
                link(nc.vector.tensor_tensor(den, den, top[:, :, 1], ALU.add))
                link(nc.vector.reciprocal(den, den))
                link(nc.vector.tensor_tensor(wts, top[:, :, 0:2], bc(den, 2), ALU.mult))
                for j in range(CT):
                    i_ = nc.vector.tensor_scalar(first[:, j], iota, idxf[:, j, 0:1], wts[:, j, 0:1], ALU.is_equal, ALU.mult)
                for j in range(CT):
                    i_ = nc.vector.tensor_scalar(comb[:, j], iota, idxf[:, j, 1:2], wts[:, j, 1:2], ALU.is_equal, ALU.mult)
                link(i_)
                nc.vector.tensor_tensor(comb, comb, first, ALU.add).then_inc(comb_sb, 1)
                dve.wait_ge(comb_sb, n + 1 + PRIME)
                assert count[0] == LINKS, count
            LINKS = 12
            for own in (xn_sb, comb_sb):
                dve.sem_inc(own, PRIME)
            dve.wait_ge(c_in, 48)
            loop(dve, body)

        @block.tensor
        def _(pe):
            for own in (y_ps, lg_ps):
                pe.sem_inc(own, PRIME)
            pe.wait_ge(c_in, 48)

            def body(n, par, i):
                pe.wait_ge(a_in[par], i * 16 + 16)
                pe.wait_ge(aT_sb, n * 2 + PRIME)
                for k in range(KD):
                    for j in range(CT):
                        m = nc.tensor.transpose(ps[:, k, j * P:(j + 1) * P], at_in[:, par, j, k * P:(k + 1) * P], ident[:, :])
                m.then_inc(aT_ps, 1)
                pe.wait_ge(aT_sb, 2 * n + 2 + PRIME)
                pe.wait_ge(xn_sb, n + PRIME)
                for j in range(CT):
                    for k in range(KD):
                        m = nc.tensor.matmul(ps[:, 2 + j // 2, (j % 2) * D:(j % 2 + 1) * D], aT[:, k, j * P:(j + 1) * P], w_o[:, k],
                                             start=k == 0, stop=k == KD - 1)
                m.then_inc(y_ps, 1)
                pe.wait_ge(xn_sb, n + 1 + PRIME)
                for k in range(KD):
                    for j in range(CT):
                        m = nc.tensor.transpose(ps[:, 4 + k, j * P:(j + 1) * P], xn[:, j, k * P:(k + 1) * P], ident[:, :])
                m.then_inc(x2_ps, 1)
                pe.wait_ge(x2_sb, 2 * n + 2)
                pe.wait_ge(comb_sb, n + PRIME)
                for j in range(CT):
                    for k in range(KD):
                        m = nc.tensor.matmul(ps[:, 6, j * NE:(j + 1) * NE], x2s[:, k, j * P:(j + 1) * P], w_r[:, k],
                                             start=k == 0, stop=k == KD - 1)
                m.then_inc(lg_ps, 1)
                pe.wait_ge(comb_sb, n + 1 + PRIME)
                pe.wait_ge(cT_sb2, n + PRIME)
                for j in range(CT):
                    m = nc.tensor.transpose(ps[0:NE, 7, j * P:(j + 1) * P], comb[:, j], ident[:, :])
                m.then_inc(cT_ps2, 1)
            loop(pe, body)

        @block.scalar
        def _(act):
            for own in (aT_sb, cT_sb2):
                act.sem_inc(own, PRIME)

            def body(n, par, i):
                act.wait_ge(aT_ps, n + 1)
                act.wait_ge(y_ps, n + PRIME)
                for k in range(KD):
                    nc.scalar.copy(aT[:, k], ps[:, k]).then_inc(aT_sb, 1)
                act.wait_ge(x2_ps, n + 1)
                act.wait_ge(lg_ps, n + PRIME)
                act.wait_ge(x2_cp, n + PRIME)
                for k in range(KD):
                    nc.scalar.copy(x2s[:, k], ps[:, 4 + k]).then_inc(x2_sb, 1)
                act.wait_ge(lsub_sb, n + 1)
                nc.scalar.activation(ex, lsub, ACT.Exp).then_inc(ex_sb, 1)
                act.wait_ge(cT_ps2, n + 1)
                nc.scalar.copy(combT[:, bass.ds(n * CH, CH)], ps[0:NE, 7]).then_inc(cT_sb2, 1)
            loop(act, body)


def ffn_weights(stack):
    big = stack[:, :, :, :].rearrange("p a b s -> p (a b s)").bitcast(F32)
    n = 2 * KD * HT * P
    w_up = big[:, 0:n].rearrange("p (i k h m) -> p i k h m", i=2, k=KD, h=HT)
    w_dn = big[:, n:n + HT * D].rearrange("p (h d) -> p h d", h=HT)
    return w_up, w_dn


def experts(nc, io, sem, ident, xT, V_all, decay, small, w_qk, part, stack, work, ps, **_):
    x1 = V_all[:, :, :, :].rearrange("p h k d -> p h (k d)")
    combT = decay[0:NE].rearrange("p a t -> p (a t)")
    w_up, w_dn = ffn_weights(stack)
    hid = carve(work, 0, 2, HT, CH)
    gate = carve(work, 10240, 2, CH)
    tail = part[:, :, :, :, :].rearrange("p a b i c -> p (a b i c)").bitcast(F32)
    zn = tail[:, 0:CT * D].rearrange("p (j d) -> p j d", j=CT)
    res = tail[:, CT * D:3 * CT * D].rearrange("p (a j d) -> p a j d", a=2, j=CT)
    sel = w_qk[0:NE].rearrange("p a k n -> p (a k n)").rearrange("p (h m) -> p h m", m=P)
    bn = carve(small, 0, CT, 6)
    mv = carve(small, 32, CT, 2)
    ve = carve(small, 48, CT)
    rs = carve(small, 56, CT)
    mhalf = carve(small, 64, CT)

    sel_in, g_ps, u_ps, c_ps, gate_sb, hu_sb, h_sb, dn_ps = (sem(n) for n in (
        "sel_in", "g_ps", "u_ps", "c_ps", "gate_sb", "hu_sb", "h_sb", "dn_ps"))
    fchain, fve, frs, fzn, fres, half3 = (sem(n) for n in ("fchain", "fve", "frs", "fzn", "fres", "half3"))
    out_done = [sem(f"out_done{i}") for i in range(2)]
    out_dram = io["out"].rearrange("b s d -> (b s) d").rearrange("(n j p) d -> p n j d", j=CT, p=P)
    NR = HT - NSH

    def loop(eng, body):
        with eng.Fori(0, NB // 2) as i:
            for par in range(2):
                body(i * 2 + par, par, i)

    with nc.Block() as block:
        @block.sync
        def _(sp):
            sp.dma_start(sel, io["c_sel"]).then_inc(sel_in, 16)

            def body(n, par, i):
                sp.wait_ge(fres, n + 1)
                sp.dma_start(out_dram[:, bass.ds(n, 1)].rearrange("p o j d -> p (o j) d"), res[:, par]).then_inc(out_done[par], 16)
            loop(sp, body)
            for par in range(2):
                sp.wait_ge(out_done[par], 16 * NB // 2 + PRIME)

        @block.gpsimd
        def _(pool):
            for par in range(2):
                pool.sem_inc(out_done[par], PRIME)
            nc.gpsimd.memset(mhalf, -0.5).then_inc(half3, 1)
            pool.wait_ge(half3, 1)

            def body(n, par, i):
                pool.wait_ge(fve, n + 1)
                nc.gpsimd.tensor_tensor(rs, ve, mhalf, ALU.pow).then_inc(frs, 1)
            loop(pool, body)

        @block.scalar
        def _(act):
            act.sem_inc(gate_sb, PRIME)

            def body(n, par, i):
                for h in range(HT):
                    act.wait_ge(g_ps, n * HT + h + 1)
                    if h >= 2:
                        act.wait_ge(hu_sb, n * HT + h - 1 + PRIME)
                    else:
                        act.wait_ge(hu_sb, n * HT + PRIME)
                    nc.scalar.activation(gate[:, h % 2], ps[:, h % 2], ACT.Silu).then_inc(gate_sb, 1)
            loop(act, body)

        @block.tensor
        def _(pe):
            pe.sem_inc(dn_ps, PRIME)
            pe.wait_ge(sel_in, 16)

            def body(n, par, i):
                for h in range(HT):
                    x = lambda k: xT[:, k, bass.ds(n * CH, CH)]
                    if h >= 2:
                        pe.wait_ge(gate_sb, n * HT + h - 1 + PRIME)
                    else:
                        pe.wait_ge(gate_sb, n * HT + PRIME)
                    for k in range(KD):
                        m = nc.tensor.matmul(ps[:, h % 2], w_up[:, 0, k, h], x(k), start=k == 0, stop=k == KD - 1)
                    m.then_inc(g_ps, 1)
                    if h >= 2:
                        pe.wait_ge(hu_sb, n * HT + h - 1 + PRIME)
                    else:
                        pe.wait_ge(hu_sb, n * HT + PRIME)
                    if h >= NSH:
                        pe.wait_ge(h_sb, n * NR + max(h - NSH - 1, 0) + PRIME)
                    for k in range(KD):
                        m = nc.tensor.matmul(ps[:, 2 + h % 2], w_up[:, 1, k, h], x(k), start=k == 0, stop=k == KD - 1)
                    m.then_inc(u_ps, 1)
                    if h >= NSH:
                        e = h - NSH
                        nc.tensor.matmul(ps[:, 4 + h % 2], sel[:, e], combT[:, bass.ds(n * CH, CH)], start=True, stop=True).then_inc(c_ps, 1)
                pe.wait_ge(h_sb, (n + 1) * NR + PRIME)
                pe.wait_ge(hu_sb, (n + 1) * HT + PRIME)
                pe.wait_ge(fzn, n + PRIME)
                for j in range(CT):
                    for h in range(HT):
                        m = nc.tensor.matmul(ps[:, 6 + j // 2, (j % 2) * D:(j % 2 + 1) * D], hid[:, par, h, j * P:(j + 1) * P], w_dn[:, h],
                                             start=h == 0, stop=h == HT - 1)
                m.then_inc(dn_ps, 1)
            loop(pe, body)

        @block.vector
        def _(dve):
            for own in (hu_sb, h_sb, fzn):
                dve.sem_inc(own, PRIME)

            def body(n, par, i):
                dve.wait_ge(dn_ps, n + PRIME)
                for h in range(HT):
                    dve.wait_ge(u_ps, n * HT + h + 1)
                    dve.wait_ge(gate_sb, n * HT + h + 1 + PRIME)
                    nc.vector.tensor_tensor(hid[:, par, h], gate[:, h % 2], ps[:, 2 + h % 2], ALU.mult).then_inc(hu_sb, 1)
                    if h >= NSH:
                        dve.wait_ge(c_ps, n * NR + h - NSH + 1)
                        dve.wait_ge(hu_sb, n * HT + h + 1 + PRIME)
                        nc.vector.tensor_tensor(hid[:, par, h], hid[:, par, h], ps[:, 4 + h % 2], ALU.mult).then_inc(h_sb, 1)
                y = lambda j: ps[:, 6 + j // 2, (j % 2) * D:(j % 2 + 1) * D]
                dve.wait_ge(dn_ps, n + 1 + PRIME)
                for j in range(CT):
                    i_ = nc.vector.bn_stats(bn[:, j], y(j))
                i_.then_inc(fchain, 1)
                dve.wait_ge(fchain, n * 2 + 1)
                nc.vector.memset(ve, LN_EPS)
                for j in range(CT):
                    i_ = nc.vector.bn_aggr(mv[:, j], bn[:, j])
                i_.then_inc(fchain, 1)
                dve.wait_ge(fchain, n * 2 + 2)
                nc.vector.tensor_tensor(ve, ve, mv[:, :, 1], ALU.add).then_inc(fve, 1)
                dve.wait_ge(frs, n + 1)
                for j in range(CT):
                    i_ = nc.vector.tensor_scalar(zn[:, j], y(j), mv[:, j, 0:1], rs[:, j:j + 1], ALU.subtract, ALU.mult)
                i_.then_inc(fzn, 1)
                dve.wait_ge(fzn, n + 1 + PRIME)
                dve.wait_ge(out_done[par], i * 16 + PRIME)
                nc.vector.tensor_tensor(res[:, par], zn, x1[:, bass.ds(n * CT, CT), :], ALU.add).then_inc(fres, 1)
            loop(dve, body)


_INS = ["L0_attn_x", "L0_attn_W_q", "L0_attn_W_k", "L0_attn_W_v", "L0_attn_W_o", "L0_attn_W_down_kv", "L0_attn_W_up_k",
        "L0_attn_W_up_v", "L0_ffn_router_w", "L0_ffn_wg_r", "L0_ffn_wu_r", "L0_ffn_wd_r", "L0_ffn_wg_s", "L0_ffn_wu_s",
        "L0_ffn_wd_s"]


def constants():
    t = np.arange(S, dtype=np.float64) - S // 2
    decay = np.exp(np.array([-DECAY, DECAY])[:, None, None] * np.broadcast_to(t, (STRIP, S)))
    s, q = np.arange(P)[:, None], np.arange(P)[None, :]
    diag = np.where(s > q, np.exp(-2 * DECAY * (s - q)), 1.0)
    sel = np.zeros((NE, HT - NSH, P))
    for e in range(NE):
        sel[e, e // EPT, (e % EPT) * MR:(e % EPT + 1) * MR] = 1.0
    out = {"c_ident": np.eye(P), "c_decay": decay, "c_diag": np.stack([diag, diag.T]), "c_sel": sel,
           "c_iota": np.tile(np.arange(NE), (P, 1))}
    return {k: np.ascontiguousarray(v, dtype=np.float32) for k, v in out.items()}


def kernel(**inputs):
    import numpy as _np
    import concourse.bacc as _bacc
    from concourse import mybir as _mybir
    from concourse.bass_utils import run_bass_kernel_spmd as _run

    nc = _bacc.Bacc("TRN2", target_bir_lowering=False, num_devices=1)
    arrays, io = {}, {}
    for name, a in [(n, _np.ascontiguousarray(inputs[n])) for n in _INS] + list(constants().items()):
        arrays[f"in_{name}"] = a
        io[name] = nc.dram_tensor(f"in_{name}", a.shape, _mybir.dt.from_np(a.dtype), kind="ExternalInput").ap()
    io["out"] = nc.dram_tensor("out_0", (B, S, D), _mybir.dt.float32, kind="ExternalOutput").ap()
    emit(nc, io)
    r = _run(nc, [arrays], core_ids=[0])
    return r.results[0]["out_0"]
```

```python
import numpy as np
import concourse.bass as bass
from concourse import mybir
from contextlib import ExitStack

F32 = mybir.dt.float32
U32 = mybir.dt.uint32
I32 = mybir.dt.int32
BF16 = mybir.dt.bfloat16
ALU = mybir.AluOpType
ACT = mybir.ActivationFunctionType
AX = mybir.AxisListType

P = 128
B, S, D = 2, 2048, 256
T = B * S
H, HD = 16, 16
LAT = 64
DECAY = 0.01
KD = D // P
STRIP = 32
KT = S // P
CH = 512
QC = S // CH
CT = CH // P
NB = T // CH
NE, MR = 16, 64
NSH, MS = 2, 128
HT = (NSH * MS + NE * MR) // P
EPT = P // MR
LN_EPS = 1e-5
TOP_EPS = 1e-9
SAFE = 60.0
PRIME = 2


def emit(nc, io):
    ctx = ExitStack()
    with ctx:
        sb = lambda n, s, d=F32: ctx.enter_context(nc.sbuf_tensor(n, s, d))
        sem = lambda n: ctx.enter_context(nc.semaphore(n))

        ident = sb("ident", [P, P])
        small = sb("small", [P, 1152])
        xT = sb("xT", [P, KD, T])
        V_all = sb("V_all", [P, B * H, KT, HD])
        decay = sb("decay", [P, 2, S])
        w_qk = sb("w_qk", [P, 2, KD, D])
        w_unit = sb("w_unit", [P, 2, KD, P])
        stack = sb("stack", [P, 2, 4, S], BF16)
        part = sb("part", [P, 2, 2, 3, CH], BF16)
        work = sb("work", [P, 13312])
        ps = ctx.enter_context(nc.psum_tensor("ps", [P, 8, CH], F32))

        dram = lambda n, s: nc.dram_tensor(n, s, F32, kind="Internal").ap()
        attn_dram = dram("attn_dram", [T, D])
        parts_dram = nc.dram_tensor("parts_dram", [4, 3, B * H, HD, S], BF16, kind="Internal").ap()

        common = dict(nc=nc, io=io, sb=sb, sem=sem, ident=ident, xT=xT, V_all=V_all, decay=decay, small=small,
                      w_qk=w_qk, w_unit=w_unit, stack=stack, part=part, work=work, ps=ps,
                      attn_dram=attn_dram, parts_dram=parts_dram)
        prologue(**common)
        attention(**common)
        router(**common)
        experts(**common)


def carve(t, at, *shape):
    n = int(np.prod(shape))
    v = t[:, at:at + n]
    names = "abcd"[:len(shape)]
    if len(shape) > 1:
        v = v.rearrange(f"p ({' '.join(names)}) -> p {' '.join(names)}", **{k: s for k, s in zip(names[1:], shape[1:])})
    return v


def prologue(nc, io, sem, ident, xT, V_all, decay, small, w_qk, work, ps, **_):
    w_k = carve(work, 0, KD, D)
    w_v = carve(work, 512, KD, D)
    w_q = carve(work, 1024, KD, D)
    w_kv = carve(work, 1536, KD, D)
    w_kvT = carve(work, 2048, KD, D)
    w_dn = carve(work, 2560, KD, LAT)
    w_uk = carve(work, 2688, D)
    w_uv = carve(work, 2944, D)
    w_cT = carve(work, 3200, D)
    w_veff = carve(work, 3456, KD, D)
    xin = carve(work, 4096, 4, CT, D)
    xn = carve(work, 8192, 2, CT, D)
    bn = carve(small, 0, NB, CT, 6)
    mv = carve(small, 192, NB, CT, 2)
    ve = carve(small, 256, NB, CT)
    rs = carve(small, 288, NB, CT)
    mhalf = carve(small, 320, CT)

    ident_in, w_in, dec_in = sem("ident_in"), sem("w_in"), sem("dec_in")
    dec_ones = sem("dec_ones")
    x_in = [sem(f"x_in{i}") for i in range(4)]
    kv_sum, kvT_ps, kvT_sb = sem("kv_sum"), sem("kvT_ps"), sem("kvT_sb")
    cT_ps, cT_sb, eff_ps, eff_sb = sem("cT_ps"), sem("cT_sb"), sem("eff_ps"), sem("eff_sb")
    stats, aggr, var_eps, rstd, xn_ready = sem("stats"), sem("aggr"), sem("var_eps"), sem("rstd"), sem("xn_ready")
    half_set, xT_ps, xT_sb, v_ps, v_sb = sem("half_set"), sem("xT_ps"), sem("xT_sb"), sem("v_ps"), sem("v_sb")
    x_dram = io["L0_attn_x"].rearrange("b s d -> (b s) d").rearrange("(n j p) d -> n p j d", j=CT, p=P)
    rows = lambda w: w.rearrange("(k p) n -> p k n", p=P)

    with nc.Block() as block:
        @block.sync
        def _(sp):
            sp.dma_start(ident[:, :], io["c_ident"]).then_inc(ident_in, 16)
            for dst, name in ((w_k, "L0_attn_W_k"), (w_v, "L0_attn_W_v"), (w_dn, "L0_attn_W_down_kv"), (w_q, "L0_attn_W_q")):
                sp.dma_start(dst, rows(io[name])).then_inc(w_in, 16)
            sp.dma_start(w_uk[0:LAT], io["L0_attn_W_up_k"]).then_inc(w_in, 16)
            sp.dma_start(w_uv[0:LAT], io["L0_attn_W_up_v"]).then_inc(w_in, 16)
            for n in range(NB):
                if n >= 4:
                    sp.wait_ge(xn_ready, n - 3)
                sp.dma_start(xin[:, n % 4], x_dram[n]).then_inc(x_in[n % 4], 16)
            for r in range(P // STRIP):
                for sign in range(2):
                    sp.dma_start(decay[STRIP * r:STRIP * (r + 1), sign, :], io["c_decay"][sign]).then_inc(dec_in, 16)
            sp.wait_ge(w_in, 6 * 16)
            sp.wait_ge(dec_in, 8 * 16)

        @block.gpsimd
        def _(pool):
            nc.gpsimd.memset(mhalf, -0.5).then_inc(half_set, 1)
            pool.wait_ge(half_set, 1)
            for n in range(NB):
                pool.wait_ge(var_eps, n + 1)
                nc.gpsimd.tensor_tensor(rs[:, n], ve[:, n], mhalf, ALU.pow).then_inc(rstd, 1)

        @block.vector
        def _(dve):
            def normalise(n):
                dve.wait_ge(rstd, n + 1)
                if n >= 2:
                    dve.wait_ge(xT_ps, 2 * (n - 1))
                for j in range(CT):
                    i = nc.vector.tensor_scalar(xn[:, n % 2, j], xin[:, n % 4, j], mv[:, n, j, 0:1],
                                                rs[:, n, j:j + 1], ALU.subtract, ALU.mult)
                i.then_inc(xn_ready, 1)

            dve.wait_ge(w_in, 6 * 16)
            nc.vector.tensor_tensor(w_kv, w_k, w_v, ALU.add).then_inc(kv_sum, 1)
            nc.vector.tensor_copy(w_qk[:, 0], w_q)
            for n in range(NB):
                dve.wait_ge(x_in[n % 4], 16 * (n // 4 + 1))
                for j in range(CT):
                    i = nc.vector.bn_stats(bn[:, n, j], xin[:, n % 4, j])
                i.then_inc(stats, 1)
                dve.wait_ge(stats, n + 1)
                for j in range(CT):
                    i = nc.vector.bn_aggr(mv[:, n, j], bn[:, n, j])
                i.then_inc(aggr, 1)
                dve.wait_ge(aggr, n + 1)
                nc.vector.tensor_scalar(ve[:, n], mv[:, n, :, 1], LN_EPS, None, ALU.add).then_inc(var_eps, 1)
                if n == 1:
                    dve.wait_ge(eff_ps, 1)
                    nc.vector.tensor_copy(w_qk[:, 1], ps[:, 2, :].rearrange("p (k n) -> p k n", k=KD))
                    nc.vector.tensor_copy(w_veff, ps[:, 3, :].rearrange("p (k n) -> p k n", k=KD)).then_inc(eff_sb, 1)
                if n >= 1:
                    normalise(n - 1)
            normalise(NB - 1)

        @block.tensor
        def _(pe):
            pe.wait_ge(ident_in, 16)
            pe.wait_ge(kv_sum, 1)
            for k in range(KD):
                for i in range(KD):
                    m = nc.tensor.transpose(ps[:, 0, k * D + i * P:k * D + (i + 1) * P], w_kv[:, i, k * P:(k + 1) * P], ident[:, :])
            m.then_inc(kvT_ps, 1)
            pe.wait_ge(kvT_sb, 1)
            for k in range(KD):
                m = nc.tensor.matmul(ps[0:LAT, 1, 0:D], w_dn[:, k], w_kvT[:, k], start=k == 0, stop=k == KD - 1)
            m.then_inc(cT_ps, 1)
            pe.wait_ge(cT_sb, 1)
            for bank, up in ((2, w_uk), (3, w_uv)):
                for k in range(KD):
                    m = nc.tensor.matmul(ps[:, bank, k * D:(k + 1) * D], w_cT[0:LAT, k * P:(k + 1) * P], up[0:LAT], start=True, stop=True)
            m.then_inc(eff_ps, 1)
            for n in range(NB):
                pe.wait_ge(xn_ready, n + 1)
                if n >= 1:
                    pe.wait_ge(xT_sb, 2 * n)
                for k in range(KD):
                    for j in range(CT):
                        m = nc.tensor.transpose(ps[:, 4 + k, j * P:(j + 1) * P], xn[:, n % 2, j, k * P:(k + 1) * P], ident[:, :])
                    m.then_inc(xT_ps, 1)
                if n == 0:
                    pe.wait_ge(eff_sb, 1)
                pe.wait_ge(xT_sb, 2 * n + 2)
                for j in range(CT):
                    if j % 2 == 0 and n >= 1:
                        pe.wait_ge(v_sb, 2 * (n - 1) + j // 2 + 1)
                    for k in range(KD):
                        at = (n * CT + j) * P
                        m = nc.tensor.matmul(ps[:, 6 + j // 2, (j % 2) * D:(j % 2 + 1) * D], xT[:, k, at:at + P],
                                             w_veff[:, k], start=k == 0, stop=k == KD - 1)
                    if j % 2:
                        m.then_inc(v_ps, 1)

        @block.scalar
        def _(act):
            act.wait_ge(kvT_ps, 1)
            nc.scalar.copy(w_kvT, ps[:, 0, :].rearrange("p (k n) -> p k n", k=KD)).then_inc(kvT_sb, 1)
            act.wait_ge(cT_ps, 1)
            nc.scalar.copy(w_cT[0:LAT], ps[0:LAT, 1, 0:D]).then_inc(cT_sb, 1)
            for n in range(NB):
                for k in range(KD):
                    act.wait_ge(xT_ps, 2 * n + k + 1)
                    nc.scalar.copy(xT[:, k, n * CH:(n + 1) * CH], ps[:, 4 + k, :]).then_inc(xT_sb, 1)
                for i in range(2):
                    act.wait_ge(v_ps, 2 * n + i + 1)
                    b, kt = divmod(n * CT + 2 * i, KT)
                    for j in range(2):
                        v = nc.scalar.copy(V_all[:, b * H:(b + 1) * H, kt + j], ps[:, 6 + i, j * D:(j + 1) * D].rearrange("p (h d) -> p h d", h=H))
                    v.then_inc(v_sb, 1)


def attention(nc, io, sb, sem, ident, xT, V_all, decay, small, w_qk, w_unit, stack, part, work, ps, attn_dram, parts_dram, **_):
    probs = carve(work, 0, 3, S)
    diag_s = carve(work, 6144, 2, S)
    Vg = carve(work, 10240, 2, KT, STRIP)
    O_sb = carve(work, 11264, CH)
    att = carve(work, 11776, KT, 2 * HD)
    split = carve(work, 12288, 2, CH)
    ones = carve(small, 960, P)
    dmask = carve(small, 0, P)
    dmaskT = carve(small, 128, P)
    rden = carve(small, 256, CT, QC)
    mpart = carve(small, 288, KT, QC)
    mneg = carve(small, 352, P)
    mrow = carve(small, 480, P)
    mleft = carve(small, 608, P)
    mrow3 = carve(small, 736, 3 * P // 2).bitcast(BF16).rearrange("p (i q) -> p i q", i=3)
    bound = carve(small, 928, 2)
    bound_new = carve(small, 930, 2)
    bound_all = carve(small, 932, 2)
    after_bd = carve(small, 934, 1)
    flags = carve(small, 936, B * H // 2 + 1).bitcast(I32)
    QL, QU, KL, KU = range(4)
    ACC = 6

    names = ("vg w proj_ps proj_free prep_link prep_sb sc_ps exp_done pv_done o_sb oT_ps rden_sb att_sb d_ps d_sb "
             "mx_ps mx_mul mx_red mx_all mx_neg mxT_ps mx_link mx_part mx_rows z_ps z_add bd bd_link bd_all flag dg dexp").split()
    s_ = {n: sem("a_" + n) for n in names}
    s_.update(att_out=sem("a_att_out"), stk0=sem("a_stk0"), stk1=sem("a_stk1"), out0=sem("a_out0"), out1=sem("a_out1"))
    cst_in, vg_set, stack_set, mneg_set = sem("cst_in"), sem("vg_set"), sem("stack_set"), sem("mneg_set")
    wait = lambda eng, name, v: eng.wait_ge(s_[name], v + PRIME)
    prime = lambda eng, *ns: [eng.sem_inc(s_[n], PRIME) for n in ns]

    NSTEP = KT
    HALF = S // 2
    NHALF = 2 * NSTEP
    NPAIR = B * H // 2
    PPU = P // HD // 2
    ROWS = 6 * HD
    SCALE = 1.0 / D ** 0.5
    chunk = lambda c: slice(c * CH, (c + 1) * CH)

    def guarded(eng, slot, body, counts):
        eng.wait_ge(cst_in, 2 * 16)
        wait(eng, "flag", slot + 1)
        flag = eng.value_load(flags[0:1, slot:slot + 1] if isinstance(slot, int) else flags[0:1, bass.ds(slot, 1)], min_val=0, max_val=1)
        with eng.If(flag == 1):
            body()
        with eng.Else():
            for name, count in counts.items():
                eng.sem_inc(s_[name], count)

    def cut(lo, hi):
        while lo < hi:
            end = min(hi, (lo // CH + 1) * CH)
            yield lo, end
            lo = end

    def score_pieces(kt, half):
        a, z = half * HALF, (half + 1) * HALF
        for lo, hi in cut(a, min(z, kt * P)):
            yield lo, hi - lo, QU, KU
        for lo, hi in cut(max(a, kt * P + P), z):
            yield lo, hi - lo, QL, KL

    def half_of(s, half):
        return 2 * ((2 * s + half) % (ACC // 2))

    def halves_read(n, s, half):
        h = 2 * s + half
        return n * NHALF + (h - 1 if h < 2 else h - 2)

    def probs_of(par, s):
        return (par * NSTEP + s) % 3

    def buffer_used(par, n, s):
        return n * NSTEP + (s - 1 if par == 0 and s < 2 else s - 2)

    def pairs(eng, pair):
        pair(0, True, True, False)
        with eng.Fori(1, NPAIR - PPU) as it:
            pair(it, True, False, False)
        with eng.Fori(NPAIR - PPU, NPAIR - 1) as it:
            pair(it, False, False, False)
        pair(NPAIR - 1, False, False, True)

    with nc.Block() as block:
        @block.sync
        def _(sp):
            sp.dma_start(dmask, io["c_diag"][0]).then_inc(cst_in, 16)
            sp.dma_start(dmaskT, io["c_diag"][1]).then_inc(cst_in, 16)

            def load_stack(m, par):
                for kind in range(4):
                    for row, pt in enumerate((0, 0, 0, 1, 1, 2) if kind in (QL, QU) else (0, 1, 2, 0, 1, 0)):
                        src = parts_dram[kind, pt, bass.ds(m, 1)].rearrange("o d s -> (o d) s")
                        sp.dma_start(stack[row * HD:(row + 1) * HD, par, kind, :], src).then_inc(s_[f"stk{par}"], 16)

            def store_parts(unit, c, which, k):
                wait(sp, "prep_sb", k + 1)
                for a in range(2):
                    kind = 2 * which + a
                    dst = parts_dram[kind].rearrange("i h d s -> i (h d) s")
                    dst = dst[:, bass.ds(unit * P, P), bass.ds(c * CH, CH)].rearrange("i r s -> r i s")
                    sp.dma_start(dst, part[:, which, a]).then_inc(s_[f"out{which}"], 16)

            def store_att(it):
                wait(sp, "att_sb", 2 * it + 2)
                dst = attn_dram.rearrange("(b t p) (u d) -> b u p t d", b=B, p=P, d=2 * HD)
                sp.dma_start(dst[bass.ds(it // (H // 2), 1), bass.ds(it % (H // 2), 1)].rearrange("b u p t d -> p (b u t) d"), att).then_inc(s_["att_out"], 16)

            def shift_rows(m, par):
                wait(sp, "mx_link", 4 * (m + 1))
                for q in (QL, QU):
                    for i in range(3):
                        dst = stack[ROWS + i:ROWS + i + 1, par, q, :].rearrange("a (t p) -> a t p", p=P)
                        sp.dma_start(dst, mrow3[0:KT, i, :]).then_inc(s_["mx_rows"], 16)

            for c in range(QC):
                for which in range(2):
                    store_parts(0, c, which, 2 * c + which)
            for which in range(2):
                wait(sp, f"out{which}", 32 * QC)
            sp.wait_ge(stack_set, 4)
            load_stack(0, 0)
            guarded(sp, 0, lambda: shift_rows(0, 0), {"mx_rows": 6 * 16})

            def pair(it, prep, first, last):
                for par in range(2):
                    n = it * 2 + par
                    end = last and par
                    if not end:
                        wait(sp, "sc_ps", n * NHALF)
                        if not first:
                            for which in range(2):
                                wait(sp, f"out{which}", ((it + par) // PPU + 1) * (32 * QC))
                        load_stack(n + 1, 1 - par)
                    if par == 0 and not first:
                        store_att(it - 1)
                    if par == 0 and prep:
                        for which in range(2):
                            store_parts(it // PPU + 1, it % PPU, which, 2 * QC + 2 * it + which)
                    if not end:
                        guarded(sp, it + par, lambda: shift_rows(n + 1, 1 - par), {"mx_rows": 6 * 16})
            pairs(sp, pair)
            store_att(NPAIR - 1)
            wait(sp, "att_out", 16 * NPAIR)

        @block.gpsimd
        def _(pool):
            prime(pool, "dg", "bd_all", "vg", "w", "att_out", "stk0", "stk1", "out0", "out1", "mx_rows")

            def values(m, par):
                nc.gpsimd.tensor_copy(Vg[:, par, :, 0:HD], V_all[:, bass.ds(m, 1)].rearrange("p o k d -> p (o k) d")).then_inc(s_["vg"], 1)

            def weights(half):
                nc.gpsimd.tensor_copy(w_unit[:, :, :, :], w_qk[:, :, :, bass.ds(half * P, P)]).then_inc(s_["w"], 1)

            weights(0)
            nc.gpsimd.memset(Vg, 0.0).then_inc(vg_set, 1)
            pool.wait_ge(vg_set, 1)
            nc.gpsimd.memset(Vg.rearrange("p a k c -> p (a k) c")[:, :, HD:HD + 1], 1.0).then_inc(vg_set, 1)
            pool.wait_ge(vg_set, 2)
            values(0, 0)

            def bounds(slot):
                wait(pool, "bd", slot + 1)
                nc.gpsimd.tensor_tensor(after_bd, bound[:, 0:1], bound[:, 1:2], ALU.mult)
                nc.gpsimd.partition_all_reduce(bound_all, bound, P, bass.bass_isa.ReduceOp.max).then_inc(s_["bd_all"], 1)

            def place_diagonal(n, par, kt):
                if kt == 0:
                    wait(pool, "dexp", n + 1)
                wait(pool, "pv_done", buffer_used(par, n, kt))
                at = slice(kt * P, (kt + 1) * P)
                nc.gpsimd.tensor_tensor(probs[:, probs_of(par, kt), at], diag_s[:, par, at], ones, ALU.mult).then_inc(s_["dg"], 1)

            nc.gpsimd.memset(ones, 1.0).then_inc(vg_set, 1)
            pool.wait_ge(vg_set, 3)
            bounds(0)

            def pair(it, prep, first, last):
                for par in range(2):
                    n = it * 2 + par
                    for kt in range(KT):
                        place_diagonal(n, par, kt)
                        if kt == 0 and par == 0 and prep:
                            wait(pool, "proj_ps", 2 * QC + 2 * it)
                            weights((it // PPU + 1) % KD)
                        if kt == 3 and not (last and par):
                            wait(pool, "pv_done", n * NSTEP)
                            values(n + 1, 1 - par)
                        if kt == KT - 4 and par == 0:
                            bounds(it + 1)
            pairs(pool, pair)

        @block.vector
        def _(dve):
            prime(dve, *"proj_free prep_link prep_sb o_sb rden_sb att_sb d_sb mx_mul mx_red mx_all mx_neg mx_link mx_part z_add bd bd_link flag".split())

            def prepare(c, which, k, bank):
                at = slice(c * CH, (c + 1) * CH) if isinstance(c, int) else bass.ds(c * CH, CH)
                pt = part[:, which]
                wait(dve, "prep_sb", k)
                wait(dve, "proj_ps", k + 1)
                wait(dve, f"out{which}", k // 2 * 32)
                nc.vector.tensor_tensor(split[:, 0], ps[:, bank], decay[:, which, at], ALU.mult)
                nc.vector.tensor_tensor(split[:, 1], ps[:, bank], decay[:, 1 - which, at], ALU.mult)
                nc.vector.tensor_reduce(bound_new[:, which:which + 1], ps[:, bank], AX.X, ALU.max, apply_absolute_value=True).then_inc(s_["proj_free"], 1)
                wait(dve, "proj_free", k + 1)
                nc.vector.tensor_tensor(bound[:, which:which + 1], bound[:, which:which + 1], bound_new[:, which:which + 1], ALU.max)
                nc.vector.tensor_copy(pt[:, :, 0], split).then_inc(s_["prep_link"], 1)
                wait(dve, "prep_link", 3 * k + 1)
                nc.vector.tensor_tensor(split, split, pt[:, :, 0], ALU.subtract).then_inc(s_["prep_link"], 1)
                wait(dve, "prep_link", 3 * k + 2)
                nc.vector.tensor_copy(pt[:, :, 1], split).then_inc(s_["prep_link"], 1)
                wait(dve, "prep_link", 3 * k + 3)
                nc.vector.tensor_tensor(pt[:, :, 2], split, pt[:, :, 1], ALU.subtract).then_inc(s_["prep_sb"], 1)

            def set_flag(slot):
                wait(dve, "bd_all", slot + 1)
                nc.vector.tensor_tensor(bound_new[:, 0:1], bound_all[:, 0:1], bound_all[:, 1:2], ALU.mult).then_inc(s_["bd_link"], 1)
                wait(dve, "bd_link", slot + 1)
                at = flags[:, slot:slot + 1] if isinstance(slot, int) else flags[:, bass.ds(slot, 1)]
                nc.vector.tensor_scalar(at, bound_new[:, 0:1], SAFE, None, ALU.is_gt).then_inc(s_["flag"], 1)

            def normalise(m, par):
                wait(dve, "pv_done", (m + 1) * NSTEP)
                nc.vector.tensor_copy(O_sb, ps[:, ACC + par]).then_inc(s_["o_sb"], 1)
                wait(dve, "oT_ps", m + 1)
                oT = ps[:, ACC + par].rearrange("p (j c d) -> p j c d", j=CT, c=QC)
                nc.vector.reciprocal(rden, oT[:, :, :, HD]).then_inc(s_["rden_sb"], 1)
                wait(dve, "rden_sb", m + 1)
                if par == 0:
                    wait(dve, "att_out", m // 2 * 16)
                dst = att[:, :, par * HD:(par + 1) * HD].rearrange("p (c j) d -> p j c d", c=QC)
                nc.vector.tensor_tensor(dst, oT[:, :, :, 0:HD], rden.unsqueeze(3).to_broadcast([P, CT, QC, HD]),
                                        ALU.mult).then_inc(s_["att_sb"], 1)

            def diagonals(m, par, bank):
                if not isinstance(m, int) or m > 1:
                    wait(dve, "dg", (m - 1) * KT)
                for c in range(QC):
                    wait(dve, "d_ps", m * QC + c + 1)
                    nc.vector.tensor_tensor(diag_s[:, par, chunk(c)].rearrange("p (j m) -> p j m", m=P),
                                            ps[:, bank].rearrange("p (j m) -> p j m", m=P),
                                            dmask.unsqueeze(1).to_broadcast([P, CT, P]), ALU.mult).then_inc(s_["d_sb"], 1)

            def maxima(m, par, bank):
                for t in range(KT):
                    for kc in range(QC):
                        wait(dve, "mx_ps", m * (KT * QC) + t * QC + kc + 1)
                        if kc == t // CT:
                            blk = ps[:, bank, t % CT * P:(t % CT + 1) * P]
                            nc.vector.tensor_tensor(blk, blk, dmaskT, ALU.mult).then_inc(s_["mx_mul"], 1)
                            wait(dve, "mx_mul", m * KT + t + 1)
                        nc.vector.tensor_reduce(mpart[:, t, kc:kc + 1], ps[:, bank], AX.X, ALU.max).then_inc(s_["mx_red"], 1)
                wait(dve, "mx_red", (m + 1) * (KT * QC))
                nc.vector.tensor_reduce(mneg[:, 0:KT], mpart, AX.X, ALU.max).then_inc(s_["mx_all"], 1)
                wait(dve, "mx_all", m + 1)
                nc.vector.tensor_scalar(mneg[:, 0:KT], mneg[:, 0:KT], -1.0, None, ALU.mult).then_inc(s_["mx_neg"], 1)
                wait(dve, "mxT_ps", m + 1)
                if not isinstance(m, int) or m:
                    wait(dve, "mx_rows", m * (6 * 16))
                nc.vector.tensor_copy(mleft[0:KT], ps[0:KT, bank, 0:P]).then_inc(s_["mx_link"], 1)
                wait(dve, "mx_link", 4 * m + 1)
                nc.vector.tensor_copy(mrow3[0:KT, 0], mleft[0:KT])
                nc.vector.tensor_copy(mrow[0:KT], mleft[0:KT]).then_inc(s_["mx_link"], 1)
                wait(dve, "mx_link", 4 * m + 2)
                nc.vector.tensor_tensor(mleft[0:KT], mrow[0:KT], mrow3[0:KT, 0], ALU.subtract).then_inc(s_["mx_link"], 1)
                wait(dve, "mx_link", 4 * m + 3)
                nc.vector.tensor_copy(mrow3[0:KT, 1], mleft[0:KT]).then_inc(s_["mx_part"], 1)
                wait(dve, "mx_part", m + 1)
                nc.vector.tensor_tensor(mrow3[0:KT, 2], mleft[0:KT], mrow3[0:KT, 1], ALU.subtract).then_inc(s_["mx_link"], 1)
                for c in range(QC):
                    wait(dve, "z_ps", m * QC + c + 1)
                    nc.vector.tensor_tensor(diag_s[:, par, chunk(c)], diag_s[:, par, chunk(c)], ps[:, bank], ALU.add).then_inc(s_["z_add"], 1)

            for par in range(2):
                nc.vector.memset(stack[ROWS:P, par, QL:QU + 1, :], 0.0).then_inc(stack_set, 1)
                nc.vector.memset(stack[ROWS:P, par, KL:KU + 1, :], 1.0).then_inc(stack_set, 1)
            nc.vector.memset(bound, 0.0)
            nc.vector.memset(mneg, 0.0).then_inc(mneg_set, 1)
            dve.wait_ge(mneg_set, 1)
            dve.wait_ge(cst_in, 2 * 16)
            for c in range(QC):
                for which in range(2):
                    prepare(c, which, 2 * c + which, ACC + 1)
            wait(dve, "prep_sb", 2 * QC)
            dve.sem_inc(s_["bd"], 1)
            counts = {"mx_mul": KT, "mx_red": KT * QC, "mx_all": 1, "mx_neg": 1, "mx_link": 4, "mx_part": 1, "z_add": QC}
            set_flag(0)
            diagonals(0, 0, ACC + 1)
            guarded(dve, 0, lambda: maxima(0, 0, ACC + 1), counts)

            def pair(it, prep, first, last):
                for par in range(2):
                    n = it * 2 + par
                    idle = ACC + 1 - par
                    if not (first and par == 0):
                        normalise(n - 1, 1 - par)
                    if par == 0 and prep:
                        for which in range(2):
                            prepare(it % PPU, which, 2 * QC + 2 * it + which, idle)
                    if par == 0:
                        wait(dve, "prep_sb", 2 * QC + 2 * it + 2 if prep else 2 * QC + 2 * (NPAIR - PPU))
                        dve.sem_inc(s_["bd"], 1)
                    else:
                        set_flag(it + 1)
                    if not (last and par):
                        diagonals(n + 1, 1 - par, idle)
                        guarded(dve, it + par, lambda: maxima(n + 1, 1 - par, idle), counts)
            pairs(dve, pair)
            normalise(B * H - 1, 1)

        @block.tensor
        def _(pe):
            prime(pe, *"proj_ps sc_ps pv_done oT_ps d_ps mx_ps mxT_ps z_ps".split())

            def project(at, which, bank):
                for k in range(KD):
                    m = nc.tensor.matmul(ps[:, bank], w_unit[:, which, k], xT[:, k, at:at + CH] if isinstance(at, int) else xT[:, k, bass.ds(at, CH)],
                                         start=k == 0, stop=k == KD - 1)
                m.then_inc(s_["proj_ps"], 1)

            def scores(par, n, s, half):
                wait(pe, "exp_done", halves_read(n, s, half))
                for q0, w, q, k in score_pieces(s, half):
                    m = nc.tensor.matmul(ps[:, half_of(s, half) + q0 // CH % 2, q0 % CH:q0 % CH + w],
                                         stack[0:ROWS + 3, par, k, s * P:(s + 1) * P],
                                         stack[0:ROWS + 3, par, q, q0:q0 + w], start=True, stop=True)
                m.then_inc(s_["sc_ps"], 1)

            def products(par, n, s):
                wait(pe, "dg", n * KT + s + 1)
                wait(pe, "exp_done", n * NHALF + 2 * s + 2)
                for c in range(QC):
                    m = nc.tensor.matmul(ps[STRIP * c:STRIP * (c + 1), ACC + par], Vg[:, par, s], probs[:, probs_of(par, s), chunk(c)],
                                         start=s == 0, stop=s == NSTEP - 1, skip_group_check=True)
                m.then_inc(s_["pv_done"], 1)

            def transposes(m, par):
                wait(pe, "o_sb", m + 1)
                for j in range(CT):
                    i = nc.tensor.transpose(ps[:, ACC + par, j * P:(j + 1) * P], O_sb[:, j * P:(j + 1) * P], ident[:, :])
                i.then_inc(s_["oT_ps"], 1)

            def diagonal(m, par, c, bank):
                for j in range(CT):
                    at = (c * CT + j) * P
                    i = nc.tensor.matmul(ps[:, bank, j * P:(j + 1) * P], stack[0:ROWS, par, KL, at:at + P],
                                         stack[0:ROWS, par, QL, at:at + P], start=True, stop=True)
                i.then_inc(s_["d_ps"], 1)

            def maxima(m, par, bank):
                for t in range(KT):
                    for kc in range(QC):
                        if t or kc:
                            wait(pe, "mx_red", m * (KT * QC) + t * QC + kc)
                        lo, hi = kc * CH, (kc + 1) * CH
                        mid = min(max((t + 1) * P, lo), hi)
                        for a, z, q, k in ((lo, mid, QL, KL), (mid, hi, QU, KU)):
                            if a < z:
                                i = nc.tensor.matmul(ps[:, bank, a - lo:z - lo], stack[0:ROWS, par, q, t * P:(t + 1) * P],
                                                     stack[0:ROWS, par, k, a:z], start=True, stop=True)
                        i.then_inc(s_["mx_ps"], 1)
                wait(pe, "mx_neg", m + 1)
                nc.tensor.transpose(ps[:, bank, 0:P], mneg, ident[:, :]).then_inc(s_["mxT_ps"], 1)
                wait(pe, "mx_link", 4 * m + 1)
                wait(pe, "mx_rows", (m + 1) * (6 * 16))
                for c in range(QC):
                    if c:
                        wait(pe, "z_add", m * QC + c)
                    nc.tensor.matmul(ps[:, bank], stack[ROWS:ROWS + 3, par, KL, 0:P], stack[ROWS:ROWS + 3, par, QL, chunk(c)],
                                     start=True, stop=True).then_inc(s_["z_ps"], 1)

            wait(pe, "w", 1)
            for k in range(2 * QC):
                if k:
                    wait(pe, "proj_free", k)
                project(k // 2 * CH, k % 2, ACC + 1)
            wait(pe, "proj_free", 2 * QC)
            wait(pe, "stk0", 24 * 16)
            for c in range(QC):
                if c:
                    wait(pe, "d_sb", c)
                diagonal(0, 0, c, ACC + 1)
            wait(pe, "d_sb", QC)
            pe.wait_ge(stack_set, 4)
            counts = {"mx_ps": KT * QC, "mxT_ps": 1, "z_ps": QC}
            guarded(pe, 0, lambda: maxima(0, 0, ACC + 1), counts)

            def pair(it, prep, first, last):
                for par in range(2):
                    n = it * 2 + par
                    idle = ACC + 1 - par
                    end = last and par
                    wait(pe, "vg", n + 1)
                    for s in range(NSTEP):
                        scores(par, n, s, 0)
                        if s >= 2:
                            products(par, n, s - 2)
                        elif not (first and par == 0):
                            products(1 - par, n - 1, NSTEP - 2 + s)
                        scores(par, n, s, 1)
                        if s == 2 and not (first and par == 0):
                            transposes(n - 1, 1 - par)
                        if par == 0 and prep:
                            at = ((it // PPU + 1) // KD) * S + (it % PPU) * CH
                            if s == 5:
                                wait(pe, "w", it + 2)
                                if not first:
                                    wait(pe, "att_sb", n)
                                project(at, 0, idle)
                            if s == 8:
                                wait(pe, "proj_free", 2 * QC + 2 * it + 1)
                                project(at, 1, idle)
                        if s >= NSTEP - QC - 1 and s < NSTEP - 1 and not end:
                            c = s - (NSTEP - QC - 1)
                            if c:
                                wait(pe, "d_sb", (n + 1) * QC + c)
                            else:
                                wait(pe, "stk" + str(1 - par), (it + 1 + par) * 384)
                                if par == 0 and prep:
                                    wait(pe, "proj_free", 2 * QC + 2 * it + 2)
                                elif not (first and par == 0):
                                    wait(pe, "att_sb", n)
                            diagonal(n + 1, 1 - par, c, idle)
                    if not end:
                        wait(pe, "d_sb", (n + 2) * QC)
                        guarded(pe, it + par, lambda: maxima(n + 1, 1 - par, idle), counts)
            pairs(pe, pair)
            for s in (NSTEP - 2, NSTEP - 1):
                products(1, B * H - 1, s)
            transposes(B * H - 1, 1)

        @block.scalar
        def _(act):
            prime(act, "exp_done", "dexp")

            def pair(it, prep, first, last):
                for par in range(2):
                    n = it * 2 + par
                    wait(act, "d_sb", (n + 1) * QC)
                    wait(act, "z_add", (n + 1) * QC)
                    nc.scalar.activation(diag_s[:, par], diag_s[:, par], ACT.Exp, scale=SCALE).then_inc(s_["dexp"], 1)
                    for s in range(NSTEP):
                        for half in range(2):
                            wait(act, "sc_ps", n * NHALF + 2 * s + half + 1)
                            if half == 0:
                                wait(act, "pv_done", buffer_used(par, n, s))
                            src = ps[:, half_of(s, half):half_of(s, half) + 2].rearrange("p a b -> p (a b)")
                            a, z = half * HALF, (half + 1) * HALF
                            own = s * P
                            parts = [(a, z)] if not a <= own < z else [x for x in ((a, own), (own + P, z)) if x[0] < x[1]]
                            for lo, hi in parts:
                                e = nc.scalar.activation(probs[:, probs_of(par, s), lo:hi], src[:, lo - a:hi - a], ACT.Exp, scale=SCALE)
                            e.then_inc(s_["exp_done"], 1)
            pairs(act, pair)


def router(nc, io, sem, ident, xT, V_all, decay, small, w_qk, stack, work, ps, attn_dram, **_):
    x1 = V_all[:, :, :, :].rearrange("p h k d -> p h (k d)")
    combT = decay[0:NE].rearrange("p a t -> p (a t)")
    at_in = carve(work, 0, 2, CT, D)
    x_in = carve(work, 2048, 2, CT, D)
    aT = carve(work, 4096, KD, CH)
    yn = carve(work, 5120, CT, D)
    xn = carve(work, 6144, CT, D)
    x1b = carve(work, 7168, CT, D)
    x2s = carve(work, 8192, KD, CH)
    w_r = carve(work, 9216, KD, NE)
    bn = carve(small, 0, CT, 6)
    mv = carve(small, 32, CT, 2)
    ve = carve(small, 48, CT)
    rs = carve(small, 56, CT)
    mhalf = carve(small, 64, CT)
    lmax = carve(small, 72, CT)
    lsub = carve(small, 80, CT, NE)
    ex = carve(small, 144, CT, NE)
    zsum = carve(small, 208, CT)
    top = carve(small, 216, CT, 8)
    den = carve(small, 248, CT)
    wts = carve(small, 256, CT, 2)
    idxf = carve(small, 272, CT, 8)
    first = carve(small, 304, CT, NE)
    comb = carve(small, 368, CT, NE)
    iota = carve(small, 432, NE)
    idx = carve(small, 448, CT, 8).bitcast(U32)

    a_in, xr_in, c_in = [sem(f"a_in{i}") for i in range(2)], [sem(f"xr_in{i}") for i in range(2)], sem("c_in")
    aT_ps, aT_sb, y_ps, dve_c, ve1, rs1, x1_sb, ve2, rs2, xn_sb = (sem(n) for n in (
        "aT_ps", "aT_sb", "y_ps", "dve_c", "ve1", "rs1", "x1_sb", "ve2", "rs2", "xn_sb"))
    x2_ps, x2_sb, x2_cp, lg_ps, lsub_sb, ex_sb, comb_sb, cT_ps2, cT_sb2, half2, x1_cp = (sem(n) for n in (
        "x2_ps", "x2_sb", "x2_cp", "lg_ps", "lsub_sb", "ex_sb", "comb_sb", "cT_ps2", "cT_sb2", "half2", "x1_cp"))
    ffn_in = sem("ffn_in")
    a_dram = attn_dram.rearrange("(n j p) d -> p n j d", j=CT, p=P)
    x_dram = io["L0_attn_x"].rearrange("b s d -> (b s) d").rearrange("(n j p) d -> p n j d", j=CT, p=P)
    w_up, w_dn = ffn_weights(stack)
    w_o = w_qk[:, 0]

    def loop(eng, body):
        with eng.Fori(0, NB // 2) as i:
            for par in range(2):
                body(i * 2 + par, par, i)

    with nc.Block() as block:
        @block.sync
        def _(sp):
            sp.dma_start(w_o, io["L0_attn_W_o"].rearrange("(k p) n -> p k n", p=P)).then_inc(c_in, 16)
            sp.dma_start(w_r, io["L0_ffn_router_w"].rearrange("(k p) n -> p k n", p=P)).then_inc(c_in, 16)
            sp.dma_start(iota, io["c_iota"]).then_inc(c_in, 16)
            sp.dma_start(at_in[:, 0], a_dram[:, 0]).then_inc(a_in[0], 16)
            sp.dma_start(x_in[:, 0], x_dram[:, 0]).then_inc(xr_in[0], 16)
            sp.dma_start(at_in[:, 1], a_dram[:, 1]).then_inc(a_in[1], 16)
            sp.dma_start(x_in[:, 1], x_dram[:, 1]).then_inc(xr_in[1], 16)
            rows = lambda w: w.rearrange("(k p) m -> p k m", p=P)
            for i, (r, s) in enumerate((("L0_ffn_wg_r", "L0_ffn_wg_s"), ("L0_ffn_wu_r", "L0_ffn_wu_s"))):
                for e in range(NSH):
                    sp.dma_start(w_up[:, i, :, e], rows(io[s][e])).then_inc(ffn_in, 16)
                for e in range(NE):
                    dst = w_up[:, i, :, NSH + e // EPT, (e % EPT) * MR:(e % EPT + 1) * MR]
                    sp.dma_start(dst, rows(io[r][e])).then_inc(ffn_in, 16)
            sp.dma_start(w_dn[:, 0:NSH], io["L0_ffn_wd_s"].rearrange("e m d -> m e d")).then_inc(ffn_in, 16)
            sp.dma_start(w_dn[:, NSH:], io["L0_ffn_wd_r"].rearrange("(h e) m d -> (e m) h d", e=EPT)).then_inc(ffn_in, 16)
            with sp.Fori(0, NB // 2 - 1) as i:
                for par in range(2):
                    n = i * 2 + par
                    sp.wait_ge(aT_ps, n + 1)
                    sp.dma_start(at_in[:, par], a_dram[:, bass.ds(n + 2, 1)].rearrange("p o j d -> p (o j) d")).then_inc(a_in[par], 16)
                    sp.wait_ge(x1_sb, n + 1)
                    sp.dma_start(x_in[:, par], x_dram[:, bass.ds(n + 2, 1)].rearrange("p o j d -> p (o j) d")).then_inc(xr_in[par], 16)
            sp.wait_ge(ffn_in, 16 * (2 * (NSH + NE) + 2))

        @block.gpsimd
        def _(pool):
            pool.sem_inc(x2_cp, PRIME)
            nc.gpsimd.memset(mhalf, -0.5).then_inc(half2, 1)
            pool.wait_ge(half2, 1)

            def body(n, par, i):
                pool.wait_ge(ve1, n + 1)
                nc.gpsimd.tensor_tensor(rs, ve, mhalf, ALU.pow).then_inc(rs1, 1)
                pool.wait_ge(ve2, n + 1)
                nc.gpsimd.tensor_tensor(rs, ve, mhalf, ALU.pow).then_inc(rs2, 1)
                pool.wait_ge(x2_sb, 2 * n + 2)
                nc.gpsimd.tensor_copy(xT[:, :, bass.ds(n * CH, CH)], x2s).then_inc(x2_cp, 1)
            loop(pool, body)

        @block.vector
        def _(dve):
            def body(n, par, i):
                count = [0]

                def link(ins):
                    count[0] += 1
                    ins.then_inc(dve_c, 1)
                    dve.wait_ge(dve_c, n * LINKS + count[0])

                def stats(src):
                    for j in range(CT):
                        i_ = nc.vector.bn_stats(bn[:, j], src(j))
                    link(i_)
                    nc.vector.memset(ve, LN_EPS)
                    for j in range(CT):
                        i_ = nc.vector.bn_aggr(mv[:, j], bn[:, j])
                    link(i_)
                    return nc.vector.tensor_tensor(ve, ve, mv[:, :, 1], ALU.add)

                y = lambda j: ps[:, 2 + j // 2, (j % 2) * D:(j % 2 + 1) * D]
                dve.wait_ge(y_ps, n + 1 + PRIME)
                stats(y).then_inc(ve1, 1)
                dve.wait_ge(rs1, n + 1)
                for j in range(CT):
                    i_ = nc.vector.tensor_scalar(yn[:, j], y(j), mv[:, j, 0:1], rs[:, j:j + 1], ALU.subtract, ALU.mult)
                link(i_)
                dve.wait_ge(xr_in[par], i * 16 + 16)
                nc.vector.tensor_tensor(x1b, yn, x_in[:, par], ALU.add).then_inc(x1_sb, 1)
                dve.wait_ge(x1_sb, n + 1)
                nc.vector.tensor_copy(x1[:, bass.ds(n * CT, CT), :], x1b)
                stats(lambda j: x1b[:, j]).then_inc(ve2, 1)
                dve.wait_ge(rs2, n + 1)
                for j in range(CT):
                    i_ = nc.vector.tensor_scalar(xn[:, j], x1b[:, j], mv[:, j, 0:1], rs[:, j:j + 1], ALU.subtract, ALU.mult)
                i_.then_inc(xn_sb, 1)
                dve.wait_ge(lg_ps, n + 1 + PRIME)
                lg = ps[:, 6, 0:CT * NE].rearrange("p (j e) -> p j e", j=CT)
                bc = lambda v, w: v.unsqueeze(2).to_broadcast([P, CT, w])
                link(nc.vector.tensor_reduce(lmax, lg, AX.X, ALU.max))
                nc.vector.tensor_tensor(lsub, lg, bc(lmax, NE), ALU.subtract).then_inc(lsub_sb, 1)
                dve.wait_ge(ex_sb, n + 1)
                nc.vector.tensor_reduce(zsum, ex, AX.X, ALU.add)
                for j in range(CT):
                    i_ = nc.vector.max(top[:, j], ex[:, j])
                link(i_)
                nc.vector.scalar_tensor_tensor(den, zsum, TOP_EPS, top[:, :, 0], ALU.mult, ALU.add)
                for j in range(CT):
                    i_ = nc.vector.max_index(idx[:, j], top[:, j], ex[:, j])
                link(i_)
                nc.vector.tensor_copy(idxf, idx)
                link(nc.vector.tensor_tensor(den, den, top[:, :, 1], ALU.add))
                link(nc.vector.reciprocal(den, den))
                link(nc.vector.tensor_tensor(wts, top[:, :, 0:2], bc(den, 2), ALU.mult))
                for j in range(CT):
                    i_ = nc.vector.tensor_scalar(first[:, j], iota, idxf[:, j, 0:1], wts[:, j, 0:1], ALU.is_equal, ALU.mult)
                for j in range(CT):
                    i_ = nc.vector.tensor_scalar(comb[:, j], iota, idxf[:, j, 1:2], wts[:, j, 1:2], ALU.is_equal, ALU.mult)
                link(i_)
                nc.vector.tensor_tensor(comb, comb, first, ALU.add).then_inc(comb_sb, 1)
                dve.wait_ge(comb_sb, n + 1 + PRIME)
                assert count[0] == LINKS, count
            LINKS = 12
            for own in (xn_sb, comb_sb):
                dve.sem_inc(own, PRIME)
            dve.wait_ge(c_in, 48)
            loop(dve, body)

        @block.tensor
        def _(pe):
            for own in (y_ps, lg_ps):
                pe.sem_inc(own, PRIME)
            pe.wait_ge(c_in, 48)

            def body(n, par, i):
                pe.wait_ge(a_in[par], i * 16 + 16)
                pe.wait_ge(aT_sb, n * 2 + PRIME)
                for k in range(KD):
                    for j in range(CT):
                        m = nc.tensor.transpose(ps[:, k, j * P:(j + 1) * P], at_in[:, par, j, k * P:(k + 1) * P], ident[:, :])
                m.then_inc(aT_ps, 1)
                pe.wait_ge(aT_sb, 2 * n + 2 + PRIME)
                pe.wait_ge(xn_sb, n + PRIME)
                for j in range(CT):
                    for k in range(KD):
                        m = nc.tensor.matmul(ps[:, 2 + j // 2, (j % 2) * D:(j % 2 + 1) * D], aT[:, k, j * P:(j + 1) * P], w_o[:, k],
                                             start=k == 0, stop=k == KD - 1)
                m.then_inc(y_ps, 1)
                pe.wait_ge(xn_sb, n + 1 + PRIME)
                for k in range(KD):
                    for j in range(CT):
                        m = nc.tensor.transpose(ps[:, 4 + k, j * P:(j + 1) * P], xn[:, j, k * P:(k + 1) * P], ident[:, :])
                m.then_inc(x2_ps, 1)
                pe.wait_ge(x2_sb, 2 * n + 2)
                pe.wait_ge(comb_sb, n + PRIME)
                for j in range(CT):
                    for k in range(KD):
                        m = nc.tensor.matmul(ps[:, 6, j * NE:(j + 1) * NE], x2s[:, k, j * P:(j + 1) * P], w_r[:, k],
                                             start=k == 0, stop=k == KD - 1)
                m.then_inc(lg_ps, 1)
                pe.wait_ge(comb_sb, n + 1 + PRIME)
                pe.wait_ge(cT_sb2, n + PRIME)
                for j in range(CT):
                    m = nc.tensor.transpose(ps[0:NE, 7, j * P:(j + 1) * P], comb[:, j], ident[:, :])
                m.then_inc(cT_ps2, 1)
            loop(pe, body)

        @block.scalar
        def _(act):
            for own in (aT_sb, cT_sb2):
                act.sem_inc(own, PRIME)

            def body(n, par, i):
                act.wait_ge(aT_ps, n + 1)
                act.wait_ge(y_ps, n + PRIME)
                for k in range(KD):
                    nc.scalar.copy(aT[:, k], ps[:, k]).then_inc(aT_sb, 1)
                act.wait_ge(x2_ps, n + 1)
                act.wait_ge(lg_ps, n + PRIME)
                act.wait_ge(x2_cp, n + PRIME)
                for k in range(KD):
                    nc.scalar.copy(x2s[:, k], ps[:, 4 + k]).then_inc(x2_sb, 1)
                act.wait_ge(lsub_sb, n + 1)
                nc.scalar.activation(ex, lsub, ACT.Exp).then_inc(ex_sb, 1)
                act.wait_ge(cT_ps2, n + 1)
                nc.scalar.copy(combT[:, bass.ds(n * CH, CH)], ps[0:NE, 7]).then_inc(cT_sb2, 1)
            loop(act, body)


def ffn_weights(stack):
    big = stack[:, :, :, :].rearrange("p a b s -> p (a b s)").bitcast(F32)
    n = 2 * KD * HT * P
    w_up = big[:, 0:n].rearrange("p (i k h m) -> p i k h m", i=2, k=KD, h=HT)
    w_dn = big[:, n:n + HT * D].rearrange("p (h d) -> p h d", h=HT)
    return w_up, w_dn


def experts(nc, io, sem, ident, xT, V_all, decay, small, w_qk, part, stack, work, ps, **_):
    x1 = V_all[:, :, :, :].rearrange("p h k d -> p h (k d)")
    combT = decay[0:NE].rearrange("p a t -> p (a t)")
    w_up, w_dn = ffn_weights(stack)
    hid = carve(work, 0, 2, HT, CH)
    gate = carve(work, 10240, 2, CH)
    tail = part[:, :, :, :, :].rearrange("p a b i c -> p (a b i c)").bitcast(F32)
    zn = tail[:, 0:CT * D].rearrange("p (j d) -> p j d", j=CT)
    res = tail[:, CT * D:3 * CT * D].rearrange("p (a j d) -> p a j d", a=2, j=CT)
    sel = w_qk[0:NE].rearrange("p a k n -> p (a k n)").rearrange("p (h m) -> p h m", m=P)
    bn = carve(small, 0, CT, 6)
    mv = carve(small, 32, CT, 2)
    ve = carve(small, 48, CT)
    rs = carve(small, 56, CT)
    mhalf = carve(small, 64, CT)

    sel_in, g_ps, u_ps, c_ps, gate_sb, hu_sb, h_sb, dn_ps = (sem(n) for n in (
        "sel_in", "g_ps", "u_ps", "c_ps", "gate_sb", "hu_sb", "h_sb", "dn_ps"))
    fchain, fve, frs, fzn, fres, half3 = (sem(n) for n in ("fchain", "fve", "frs", "fzn", "fres", "half3"))
    out_done = [sem(f"out_done{i}") for i in range(2)]
    out_dram = io["out"].rearrange("b s d -> (b s) d").rearrange("(n j p) d -> p n j d", j=CT, p=P)
    NR = HT - NSH

    def loop(eng, body):
        with eng.Fori(0, NB // 2) as i:
            for par in range(2):
                body(i * 2 + par, par, i)

    with nc.Block() as block:
        @block.sync
        def _(sp):
            sp.dma_start(sel, io["c_sel"]).then_inc(sel_in, 16)

            def body(n, par, i):
                sp.wait_ge(fres, n + 1)
                sp.dma_start(out_dram[:, bass.ds(n, 1)].rearrange("p o j d -> p (o j) d"), res[:, par]).then_inc(out_done[par], 16)
            loop(sp, body)
            for par in range(2):
                sp.wait_ge(out_done[par], 16 * NB // 2 + PRIME)

        @block.gpsimd
        def _(pool):
            for par in range(2):
                pool.sem_inc(out_done[par], PRIME)
            nc.gpsimd.memset(mhalf, -0.5).then_inc(half3, 1)
            pool.wait_ge(half3, 1)

            def body(n, par, i):
                pool.wait_ge(fve, n + 1)
                nc.gpsimd.tensor_tensor(rs, ve, mhalf, ALU.pow).then_inc(frs, 1)
            loop(pool, body)

        @block.scalar
        def _(act):
            act.sem_inc(gate_sb, PRIME)

            def body(n, par, i):
                for h in range(HT):
                    act.wait_ge(g_ps, n * HT + h + 1)
                    if h >= 2:
                        act.wait_ge(hu_sb, n * HT + h - 1 + PRIME)
                    else:
                        act.wait_ge(hu_sb, n * HT + PRIME)
                    nc.scalar.activation(gate[:, h % 2], ps[:, h % 2], ACT.Silu).then_inc(gate_sb, 1)
            loop(act, body)

        @block.tensor
        def _(pe):
            pe.sem_inc(dn_ps, PRIME)
            pe.wait_ge(sel_in, 16)

            def body(n, par, i):
                for h in range(HT):
                    x = lambda k: xT[:, k, bass.ds(n * CH, CH)]
                    if h >= 2:
                        pe.wait_ge(gate_sb, n * HT + h - 1 + PRIME)
                    else:
                        pe.wait_ge(gate_sb, n * HT + PRIME)
                    for k in range(KD):
                        m = nc.tensor.matmul(ps[:, h % 2], w_up[:, 0, k, h], x(k), start=k == 0, stop=k == KD - 1)
                    m.then_inc(g_ps, 1)
                    if h >= 2:
                        pe.wait_ge(hu_sb, n * HT + h - 1 + PRIME)
                    else:
                        pe.wait_ge(hu_sb, n * HT + PRIME)
                    if h >= NSH:
                        pe.wait_ge(h_sb, n * NR + max(h - NSH - 1, 0) + PRIME)
                    for k in range(KD):
                        m = nc.tensor.matmul(ps[:, 2 + h % 2], w_up[:, 1, k, h], x(k), start=k == 0, stop=k == KD - 1)
                    m.then_inc(u_ps, 1)
                    if h >= NSH:
                        e = h - NSH
                        nc.tensor.matmul(ps[:, 4 + h % 2], sel[:, e], combT[:, bass.ds(n * CH, CH)], start=True, stop=True).then_inc(c_ps, 1)
                pe.wait_ge(h_sb, (n + 1) * NR + PRIME)
                pe.wait_ge(hu_sb, (n + 1) * HT + PRIME)
                pe.wait_ge(fzn, n + PRIME)
                for j in range(CT):
                    for h in range(HT):
                        m = nc.tensor.matmul(ps[:, 6 + j // 2, (j % 2) * D:(j % 2 + 1) * D], hid[:, par, h, j * P:(j + 1) * P], w_dn[:, h],
                                             start=h == 0, stop=h == HT - 1)
                m.then_inc(dn_ps, 1)
            loop(pe, body)

        @block.vector
        def _(dve):
            for own in (hu_sb, h_sb, fzn):
                dve.sem_inc(own, PRIME)

            def body(n, par, i):
                dve.wait_ge(dn_ps, n + PRIME)
                for h in range(HT):
                    dve.wait_ge(u_ps, n * HT + h + 1)
                    dve.wait_ge(gate_sb, n * HT + h + 1 + PRIME)
                    nc.vector.tensor_tensor(hid[:, par, h], gate[:, h % 2], ps[:, 2 + h % 2], ALU.mult).then_inc(hu_sb, 1)
                    if h >= NSH:
                        dve.wait_ge(c_ps, n * NR + h - NSH + 1)
                        dve.wait_ge(hu_sb, n * HT + h + 1 + PRIME)
                        nc.vector.tensor_tensor(hid[:, par, h], hid[:, par, h], ps[:, 4 + h % 2], ALU.mult).then_inc(h_sb, 1)
                y = lambda j: ps[:, 6 + j // 2, (j % 2) * D:(j % 2 + 1) * D]
                dve.wait_ge(dn_ps, n + 1 + PRIME)
                for j in range(CT):
                    i_ = nc.vector.bn_stats(bn[:, j], y(j))
                i_.then_inc(fchain, 1)
                dve.wait_ge(fchain, n * 2 + 1)
                nc.vector.memset(ve, LN_EPS)
                for j in range(CT):
                    i_ = nc.vector.bn_aggr(mv[:, j], bn[:, j])
                i_.then_inc(fchain, 1)
                dve.wait_ge(fchain, n * 2 + 2)
                nc.vector.tensor_tensor(ve, ve, mv[:, :, 1], ALU.add).then_inc(fve, 1)
                dve.wait_ge(frs, n + 1)
                for j in range(CT):
                    i_ = nc.vector.tensor_scalar(zn[:, j], y(j), mv[:, j, 0:1], rs[:, j:j + 1], ALU.subtract, ALU.mult)
                i_.then_inc(fzn, 1)
                dve.wait_ge(fzn, n + 1 + PRIME)
                dve.wait_ge(out_done[par], i * 16 + PRIME)
                nc.vector.tensor_tensor(res[:, par], zn, x1[:, bass.ds(n * CT, CT), :], ALU.add).then_inc(fres, 1)
            loop(dve, body)


_INS = ["L0_attn_x", "L0_attn_W_q", "L0_attn_W_k", "L0_attn_W_v", "L0_attn_W_o", "L0_attn_W_down_kv", "L0_attn_W_up_k",
        "L0_attn_W_up_v", "L0_ffn_router_w", "L0_ffn_wg_r", "L0_ffn_wu_r", "L0_ffn_wd_r", "L0_ffn_wg_s", "L0_ffn_wu_s",
        "L0_ffn_wd_s"]


def constants():
    t = np.arange(S, dtype=np.float64) - S // 2
    decay = np.exp(np.array([-DECAY, DECAY])[:, None, None] * np.broadcast_to(t, (STRIP, S)))
    s, q = np.arange(P)[:, None], np.arange(P)[None, :]
    diag = np.where(s > q, np.exp(-2 * DECAY * (s - q)), 1.0)
    sel = np.zeros((NE, HT - NSH, P))
    for e in range(NE):
        sel[e, e // EPT, (e % EPT) * MR:(e % EPT + 1) * MR] = 1.0
    out = {"c_ident": np.eye(P), "c_decay": decay, "c_diag": np.stack([diag, diag.T]), "c_sel": sel,
           "c_iota": np.tile(np.arange(NE), (P, 1))}
    return {k: np.ascontiguousarray(v, dtype=np.float32) for k, v in out.items()}


def kernel(**inputs):
    import numpy as _np
    import concourse.bacc as _bacc
    from concourse import mybir as _mybir
    from concourse.bass_utils import run_bass_kernel_spmd as _run

    nc = _bacc.Bacc("TRN2", target_bir_lowering=False, num_devices=1)
    arrays, io = {}, {}
    for name, a in [(n, _np.ascontiguousarray(inputs[n])) for n in _INS] + list(constants().items()):
        arrays[f"in_{name}"] = a
        io[name] = nc.dram_tensor(f"in_{name}", a.shape, _mybir.dt.from_np(a.dtype), kind="ExternalInput").ap()
    io["out"] = nc.dram_tensor("out_0", (B, S, D), _mybir.dt.float32, kind="ExternalOutput").ap()
    emit(nc, io)
    r = _run(nc, [arrays], core_ids=[0])
    return r.results[0]["out_0"]
```

```python
import numpy as np
import concourse.bass as bass
from concourse import mybir
from contextlib import ExitStack

F32 = mybir.dt.float32
U32 = mybir.dt.uint32
I32 = mybir.dt.int32
BF16 = mybir.dt.bfloat16
ALU = mybir.AluOpType
ACT = mybir.ActivationFunctionType
AX = mybir.AxisListType

P = 128
B, S, D = 2, 2048, 256
T = B * S
H, HD = 16, 16
LAT = 64
DECAY = 0.01
KD = D // P
STRIP = 32
KT = S // P
CH = 512
QC = S // CH
CT = CH // P
NB = T // CH
NE, MR = 16, 64
NSH, MS = 2, 128
HT = (NSH * MS + NE * MR) // P
EPT = P // MR
LN_EPS = 1e-5
TOP_EPS = 1e-9
SAFE = 60.0
STACK_ROWS = 6 * HD
STACK_DMAS = 12
BF16_ONES = float(np.array([0x3F803F80], np.uint32).view(np.float32)[0])
PRIME = 2


def emit(nc, io):
    ctx = ExitStack()
    with ctx:
        sb = lambda n, s, d=F32: ctx.enter_context(nc.sbuf_tensor(n, s, d))
        sem = lambda n: ctx.enter_context(nc.semaphore(n))

        ident = sb("ident", [P, P])
        small = sb("small", [P, 2096])
        xT = sb("xT", [P, KD, T])
        V_all = sb("V_all", [P, B * H, KT, HD])
        decay = sb("decay", [P, 2, S])
        w_qk = sb("w_qk", [P, 2, KD, D])
        w_unit = sb("w_unit", [P, 2, KD, P])
        stack = sb("stack", [P, 2, 4, S], BF16)
        part = sb("part", [P, 2, 2, 3, CH], BF16)
        work = sb("work", [P, 17408])
        ps = ctx.enter_context(nc.psum_tensor("ps", [P, 8, CH], F32))

        dram = lambda n, s: nc.dram_tensor(n, s, F32, kind="Internal").ap()
        attn_dram = dram("attn_dram", [T, D])
        parts_dram = nc.dram_tensor("parts_dram", [4, 3, B * H, HD, S], BF16, kind="Internal").ap()

        common = dict(nc=nc, io=io, sem=sem, ident=ident, xT=xT, V_all=V_all, decay=decay, small=small,
                      w_qk=w_qk, w_unit=w_unit, stack=stack, part=part, work=work, ps=ps,
                      attn_dram=attn_dram, parts_dram=parts_dram)
        prologue(**common)
        layer(**common)


def carve(t, at, *shape):
    n = int(np.prod(shape))
    v = t[:, at:at + n]
    names = "abcd"[:len(shape)]
    if len(shape) > 1:
        v = v.rearrange(f"p ({' '.join(names)}) -> p {' '.join(names)}", **{k: s for k, s in zip(names[1:], shape[1:])})
    return v


def diagonal_masks(small):
    return carve(small, 1840, P), carve(small, 1968, P)


def chunk_at(c):
    return slice(c * CH, (c + 1) * CH) if isinstance(c, int) else bass.ds(c * CH, CH)


def store_parts(sp, parts_dram, part, rows, cols, which, done):
    for a in range(2):
        dst = parts_dram[2 * which + a].rearrange("i h d s -> i (h d) s")[:, rows, cols]
        sp.dma_start(dst.rearrange("i r s -> r i s"), part[:, which, a]).then_inc(done, 16)


def load_stack(sp, stack, parts_dram, m, par, done):
    for kind in range(4):
        src = parts_dram[kind].rearrange("i h d s -> i (h d) s")[:, bass.ds(m * HD, HD)]
        for pt, row, count in ((0, 0, 3), (1, 3, 2), (2, 5, 1)):
            parts = src[pt:pt + 1].to_broadcast([count, HD, S]) if kind < 2 else src[0:count]
            sp.dma_start(stack[row * HD:(row + count) * HD, par, kind, :], parts).then_inc(done, 16)


def prologue(nc, io, sem, ident, xT, V_all, decay, small, w_qk, w_unit, stack, part, work, ps, parts_dram, **_):
    w_k = carve(work, 0, KD, D)
    w_v = carve(work, 512, KD, D)
    w_q = carve(work, 1024, KD, D)
    w_kv = carve(work, 1536, KD, D)
    w_kvT = carve(work, 2048, KD, D)
    w_dn = carve(work, 2560, KD, LAT)
    w_uk = carve(work, 2688, D)
    w_uv = carve(work, 2944, D)
    w_cT = carve(work, 3200, D)
    w_veff = carve(work, 3456, KD, D)
    xin = carve(work, 4096, 4, CT, D)
    xn = carve(work, 8192, 2, CT, D)
    bn = carve(small, 0, NB, CT, 6)
    mv = carve(small, 192, NB, CT, 2)
    ve = carve(small, 256, NB, CT)
    rs = carve(small, 288, NB, CT)
    mhalf = carve(small, 320, CT)
    neg_mean = carve(small, 324, NB, CT)
    shift = carve(small, 356, NB, CT)
    bound = carve(small, 928, 2)
    bound_new = carve(small, 930, 2)
    split = carve(work, 12288, 2, CH)

    ident_in, w_in, dec_in = sem("ident_in"), sem("w_in"), sem("dec_in")
    x_in = [sem(f"x_in{i}") for i in range(4)]
    kv_sum, kvT_ps, kvT_sb = sem("kv_sum"), sem("kvT_ps"), sem("kvT_sb")
    cT_ps, cT_sb, eff_ps, eff_sb = sem("cT_ps"), sem("cT_sb"), sem("eff_ps"), sem("eff_sb")
    stats, aggr, var_eps, rstd, xn_ready = sem("stats"), sem("aggr"), sem("var_eps"), sem("rstd"), sem("xn_ready")
    proj_ps, proj_free, prep_link, prep_sb, w_set, bound_set, rows_set, shift_c, stack_in = (sem("p_" + n) for n in (
        "proj_ps", "proj_free", "prep_link", "prep_sb", "w_set", "bound_set", "rows_set", "shift_c", "stack_in"))
    parts_out = [sem(f"p_out{i}") for i in range(2)]
    half_set, xT_ps, xT_sb, v_ps, v_sb = sem("half_set"), sem("xT_ps"), sem("xT_sb"), sem("v_ps"), sem("v_sb")
    x_dram = io["L0_attn_x"].rearrange("b s d -> (b s) d").rearrange("(n j p) d -> n p j d", j=CT, p=P)
    rows = lambda w: w.rearrange("(k p) n -> p k n", p=P)

    with nc.Block() as block:
        @block.sync
        def _(sp):
            sp.dma_start(ident[:, :], io["c_ident"]).then_inc(ident_in, 16)
            for dst, name in ((w_k, "L0_attn_W_k"), (w_v, "L0_attn_W_v"), (w_dn, "L0_attn_W_down_kv"), (w_q, "L0_attn_W_q")):
                sp.dma_start(dst, rows(io[name])).then_inc(w_in, 16)
            sp.dma_start(w_uk[0:LAT], io["L0_attn_W_up_k"]).then_inc(w_in, 16)
            sp.dma_start(w_uv[0:LAT], io["L0_attn_W_up_v"]).then_inc(w_in, 16)
            def load_block(n):
                if n >= 4:
                    sp.wait_ge(xn_ready, n - 3)
                sp.dma_start(xin[:, n % 4], x_dram[n]).then_inc(x_in[n % 4], 16)

            for n in range(4):
                load_block(n)
            for r in range(P // STRIP):
                for sign in range(2):
                    sp.dma_start(decay[STRIP * r:STRIP * (r + 1), sign, :], io["c_decay"][sign]).then_inc(dec_in, 16)
            for mask, dst in enumerate(diagonal_masks(small)):
                sp.dma_start(dst, io["c_diag"][mask]).then_inc(dec_in, 16)
            for n in range(4, NB):
                load_block(n)
            for k in range(2 * QC):
                sp.wait_ge(prep_sb, k + 1)
                c, which = divmod(k, 2)
                store_parts(sp, parts_dram, part, slice(0, P), chunk_at(c), which, parts_out[which])
            for which in range(2):
                sp.wait_ge(parts_out[which], 2 * 16 * QC)
            load_stack(sp, stack, parts_dram, 0, 0, stack_in)
            sp.wait_ge(w_in, 6 * 16)
            sp.wait_ge(dec_in, 10 * 16)
            sp.wait_ge(stack_in, 16 * STACK_DMAS)

        @block.gpsimd
        def _(pool):
            nc.gpsimd.memset(mhalf, -0.5).then_inc(half_set, 1)
            pool.wait_ge(half_set, 1)
            for n in range(NB):
                pool.wait_ge(var_eps, n + 1)
                nc.gpsimd.tensor_tensor(rs[:, n], ve[:, n], mhalf, ALU.pow).then_inc(shift_c, 1)
                pool.wait_ge(shift_c, n + 1)
                nc.gpsimd.tensor_tensor(shift[:, n], neg_mean[:, n], rs[:, n], ALU.mult).then_inc(rstd, 1)
                if n == 1:
                    pool.wait_ge(eff_sb, 1)
                    nc.gpsimd.tensor_copy(w_unit[:, :, :, :], w_qk[:, :, :, 0:P]).then_inc(w_set, 1)
                if n >= NB - 4:
                    if n == NB - 4:
                        pool.wait_ge(w_set, 1)
                    pool.wait_ge(rstd, n + 1)
                    par, kind, value = ((0, 0, 0.0), (0, 2, BF16_ONES), (1, 0, 0.0), (1, 2, BF16_ONES))[n - (NB - 4)]
                    rows = stack[STACK_ROWS:P, par, kind:kind + 2, :].rearrange("p a s -> p (a s)").bitcast(F32)
                    nc.gpsimd.memset(rows, value).then_inc(rows_set, 1)
                    pool.wait_ge(rows_set, n - (NB - 4) + 1)

        @block.vector
        def _(dve):
            def prepare(k):
                c, which = divmod(k, 2)
                pt = part[:, which]
                src = ps[:, k % 4]
                dve.wait_ge(proj_ps, k + 1)
                if k >= 1:
                    dve.wait_ge(prep_sb, k)
                if k >= 2:
                    dve.wait_ge(parts_out[which], 2 * 16 * (k // 2))
                nc.vector.tensor_tensor(split[:, 0], src, decay[:, which, chunk_at(c)], ALU.mult)
                nc.vector.tensor_tensor(split[:, 1], src, decay[:, 1 - which, chunk_at(c)], ALU.mult)
                nc.vector.tensor_reduce(bound_new[:, which:which + 1], src, AX.X, ALU.max, apply_absolute_value=True).then_inc(proj_free, 1)
                dve.wait_ge(proj_free, k + 1)
                nc.vector.tensor_tensor(bound[:, which:which + 1], bound[:, which:which + 1], bound_new[:, which:which + 1], ALU.max)
                nc.vector.tensor_copy(pt[:, :, 0], split).then_inc(prep_link, 1)
                dve.wait_ge(prep_link, 3 * k + 1)
                nc.vector.tensor_tensor(split, split, pt[:, :, 0], ALU.subtract).then_inc(prep_link, 1)
                dve.wait_ge(prep_link, 3 * k + 2)
                nc.vector.tensor_copy(pt[:, :, 1], split).then_inc(prep_link, 1)
                dve.wait_ge(prep_link, 3 * k + 3)
                nc.vector.tensor_tensor(pt[:, :, 2], split, pt[:, :, 1], ALU.subtract).then_inc(prep_sb, 1)

            nc.vector.memset(bound, 0.0).then_inc(bound_set, 1)
            dve.wait_ge(bound_set, 1)
            dve.wait_ge(w_in, 6 * 16)
            nc.vector.tensor_tensor(w_kv, w_k, w_v, ALU.add).then_inc(kv_sum, 1)
            nc.vector.tensor_copy(w_qk[:, 0], w_q)
            for n in range(NB):
                dve.wait_ge(x_in[n % 4], 16 * (n // 4 + 1))
                for j in range(CT):
                    i = nc.vector.bn_stats(bn[:, n, j], xin[:, n % 4, j])
                i.then_inc(stats, 1)
                dve.wait_ge(stats, n + 1)
                for j in range(CT):
                    i = nc.vector.bn_aggr(mv[:, n, j], bn[:, n, j])
                i.then_inc(aggr, 1)
                dve.wait_ge(aggr, n + 1)
                nc.vector.tensor_scalar(neg_mean[:, n], mv[:, n, :, 0], -1.0, None, ALU.mult)
                nc.vector.tensor_scalar(ve[:, n], mv[:, n, :, 1], LN_EPS, None, ALU.add).then_inc(var_eps, 1)
                if n == 1:
                    dve.wait_ge(eff_ps, 1)
                    nc.vector.tensor_copy(w_qk[:, 1], ps[:, 2, :].rearrange("p (k n) -> p k n", k=KD))
                    nc.vector.tensor_copy(w_veff, ps[:, 3, :].rearrange("p (k n) -> p k n", k=KD)).then_inc(eff_sb, 1)
                if n >= 3:
                    if n == 3:
                        dve.wait_ge(dec_in, 10 * 16)
                    prepare(n - 3)
            for k in range(NB - 3, 2 * QC):
                prepare(k)

        @block.tensor
        def _(pe):
            pe.wait_ge(ident_in, 16)
            pe.wait_ge(kv_sum, 1)
            for k in range(KD):
                for i in range(KD):
                    m = nc.tensor.transpose(ps[:, 0, k * D + i * P:k * D + (i + 1) * P], w_kv[:, i, k * P:(k + 1) * P], ident[:, :])
            m.then_inc(kvT_ps, 1)
            pe.wait_ge(kvT_sb, 1)
            for k in range(KD):
                m = nc.tensor.matmul(ps[0:LAT, 1, 0:D], w_dn[:, k], w_kvT[:, k], start=k == 0, stop=k == KD - 1)
            m.then_inc(cT_ps, 1)
            pe.wait_ge(cT_sb, 1)
            for bank, up in ((2, w_uk), (3, w_uv)):
                for k in range(KD):
                    m = nc.tensor.matmul(ps[:, bank, k * D:(k + 1) * D], w_cT[0:LAT, k * P:(k + 1) * P], up[0:LAT], start=True, stop=True)
            m.then_inc(eff_ps, 1)

            def transposes(n):
                pe.wait_ge(xn_ready, n + 1)
                if n >= 1:
                    pe.wait_ge(xT_sb, 2 * n)
                for k in range(KD):
                    for j in range(CT):
                        m = nc.tensor.transpose(ps[:, 4 + k, j * P:(j + 1) * P], xn[:, n % 2, j, k * P:(k + 1) * P], ident[:, :])
                    m.then_inc(xT_ps, 1)

            transposes(0)
            for n in range(NB):
                if n == 0:
                    pe.wait_ge(eff_sb, 1)
                pe.wait_ge(xT_sb, 2 * n + 2)
                for j in range(CT):
                    if j % 2 == 0 and n >= 1:
                        pe.wait_ge(v_sb, 2 * (n - 1) + j // 2 + 1)
                    if j == 2 and n < NB - 1:
                        transposes(n + 1)
                    for k in range(KD):
                        at = (n * CT + j) * P
                        m = nc.tensor.matmul(ps[:, 6 + j // 2, (j % 2) * D:(j % 2 + 1) * D], xT[:, k, at:at + P],
                                             w_veff[:, k], start=k == 0, stop=k == KD - 1)
                    if j % 2:
                        m.then_inc(v_ps, 1)
                if n < QC:
                    for which in range(2):
                        i = 2 * n + which
                        if i == 0:
                            pe.wait_ge(w_set, 1)
                        if i >= 4:
                            pe.wait_ge(proj_free, i - 3)
                        for k in range(KD):
                            m = nc.tensor.matmul(ps[:, i % 4], w_unit[:, which, k], xT[:, k, n * CH:(n + 1) * CH], start=k == 0, stop=k == KD - 1)
                        m.then_inc(proj_ps, 1)

        @block.scalar
        def _(act):
            act.wait_ge(kvT_ps, 1)
            nc.scalar.copy(w_kvT, ps[:, 0, :].rearrange("p (k n) -> p k n", k=KD)).then_inc(kvT_sb, 1)
            act.wait_ge(cT_ps, 1)
            nc.scalar.copy(w_cT[0:LAT], ps[0:LAT, 1, 0:D]).then_inc(cT_sb, 1)

            def normalise(n):
                act.wait_ge(rstd, n + 1)
                if n >= 2:
                    act.wait_ge(xT_ps, 2 * (n - 1))
                for j in range(CT):
                    i = nc.scalar.activation(xn[:, n % 2, j], xin[:, n % 4, j], ACT.Identity, bias=shift[:, n, j:j + 1], scale=rs[:, n, j:j + 1])
                i.then_inc(xn_ready, 1)

            normalise(0)
            for n in range(NB):
                if n < NB - 1:
                    normalise(n + 1)
                for k in range(KD):
                    act.wait_ge(xT_ps, 2 * n + k + 1)
                    nc.scalar.copy(xT[:, k, n * CH:(n + 1) * CH], ps[:, 4 + k, :]).then_inc(xT_sb, 1)
                for i in range(2):
                    act.wait_ge(v_ps, 2 * n + i + 1)
                    b, kt = divmod(n * CT + 2 * i, KT)
                    for j in range(2):
                        v = nc.scalar.copy(V_all[:, b * H:(b + 1) * H, kt + j], ps[:, 6 + i, j * D:(j + 1) * D].rearrange("p (h d) -> p h d", h=H))
                    v.then_inc(v_sb, 1)


def attention(nc, sem, ident, xT, V_all, decay, small, w_qk, w_unit, stack, part, work, ps, attn_dram, parts_dram, first_block, **_):
    probs = carve(work, 0, 3, S)
    diag_s = carve(work, 6144, 2, S)
    Vg = carve(work, 10240, 2, KT, STRIP)
    O_sb = carve(work, 11264, CH)
    att = carve(work, 11776, KT, 2 * HD)
    split = carve(work, 12288, 2, CH)
    ones = carve(small, 960, P)
    dmask, dmaskT = diagonal_masks(small)
    rden = carve(small, 256, CT, QC)
    mpart = carve(small, 288, KT, QC)
    mneg = carve(small, 352, P)
    mrow = carve(small, 480, P)
    mleft = carve(small, 608, P)
    mrow3 = carve(small, 736, 3 * P // 2).bitcast(BF16).rearrange("p (i q) -> p i q", i=3)
    bound = carve(small, 928, 2)
    bound_new = carve(small, 930, 2)
    bound_all = carve(small, 932, 2)
    after_bd = carve(small, 934, 1)
    flags = carve(small, 936, B * H // 2 + 1).bitcast(I32)
    QL, QU, KL, KU = range(4)
    ACC = 6

    names = ("vg w proj_ps proj_free prep_link prep_sb sc_ps exp_done pv_done o_sb oT_ps rden_sb att_sb d_ps d_sb "
             "mx_ps mx_mul mx_red mx_all mx_neg mxT_ps mx_link mx_part mx_rows z_ps z_add bd bd_link bd_all flag dg dexp").split()
    s_ = {n: sem("a_" + n) for n in names}
    s_.update(att_out=sem("a_att_out"), stk0=sem("a_stk0"), stk1=sem("a_stk1"), out0=sem("a_out0"), out1=sem("a_out1"))
    vg_set, mneg_set = sem("vg_set"), sem("mneg_set")
    wait = lambda eng, name, v: eng.wait_ge(s_[name], v + PRIME)
    prime = lambda eng, *ns: [eng.sem_inc(s_[n], PRIME) for n in ns]

    NSTEP = KT
    HALF = S // 2
    NHALF = 2 * NSTEP
    NPAIR = B * H // 2
    PPU = P // HD // 2
    ROWS = 6 * HD
    SCALE = 1.0 / D ** 0.5
    chunk = lambda c: slice(c * CH, (c + 1) * CH)

    def guarded(eng, slot, body, counts):
        eng.wait_ge(mneg_set, 1)
        wait(eng, "flag", slot + 1)
        flag = eng.value_load(flags[0:1, slot:slot + 1] if isinstance(slot, int) else flags[0:1, bass.ds(slot, 1)], min_val=0, max_val=1)
        with eng.If(flag == 1):
            body()
        with eng.Else():
            for name, count in counts.items():
                eng.sem_inc(s_[name], count)

    def cut(lo, hi):
        while lo < hi:
            end = min(hi, (lo // CH + 1) * CH)
            yield lo, end
            lo = end

    def score_pieces(kt, half):
        a, z = half * HALF, (half + 1) * HALF
        for lo, hi in cut(a, min(z, kt * P)):
            yield lo, hi - lo, QU, KU
        for lo, hi in cut(max(a, kt * P + P), z):
            yield lo, hi - lo, QL, KL

    def half_of(s, half):
        return 2 * ((2 * s + half) % (ACC // 2))

    def halves_read(n, s, half):
        h = 2 * s + half
        return n * NHALF + (h - 1 if h < 2 else h - 2)

    def probs_of(par, s):
        return (par * NSTEP + s) % 3

    def buffer_used(par, n, s):
        return n * NSTEP + (s - 1 if par == 0 and s < 2 else s - 2)

    def pairs(eng, pair):
        pair(0, True, True, False)
        with eng.Fori(1, NPAIR - PPU) as it:
            pair(it, True, False, False)
        with eng.Fori(NPAIR - PPU, NPAIR - 1) as it:
            pair(it, False, False, False)
        pair(NPAIR - 1, False, False, True)

    with nc.Block() as block:
        @block.sync
        def _(sp):
            def store_att(it):
                wait(sp, "att_sb", 2 * it + 2)
                dst = attn_dram.rearrange("(b t p) (u d) -> b u p t d", b=B, p=P, d=2 * HD)
                sp.dma_start(dst[bass.ds(it // (H // 2), 1), bass.ds(it % (H // 2), 1)].rearrange("b u p t d -> p (b u t) d"), att).then_inc(s_["att_out"], 16)

            def shift_rows(m, par):
                wait(sp, "mx_link", 4 * (m + 1))
                for q in (QL, QU):
                    for i in range(3):
                        dst = stack[ROWS + i:ROWS + i + 1, par, q, :].rearrange("a (t p) -> a t p", p=P)
                        sp.dma_start(dst, mrow3[0:KT, i, :]).then_inc(s_["mx_rows"], 16)

            guarded(sp, 0, lambda: shift_rows(0, 0), {"mx_rows": 6 * 16})

            def pair(it, prep, first, last):
                for par in range(2):
                    n = it * 2 + par
                    end = last and par
                    if not end:
                        wait(sp, "sc_ps", n * NHALF)
                        if not first:
                            for which in range(2):
                                wait(sp, f"out{which}", (it + par) // PPU * (32 * QC))
                        load_stack(sp, stack, parts_dram, n + 1, 1 - par, s_[f"stk{1 - par}"])
                    if par == 0 and not first:
                        store_att(it - 1)
                    if end:
                        wait(sp, "att_out", 16 * H // 2)
                        wait(sp, "w", NPAIR - PPU)
                        wait(sp, "proj_ps", 2 * (NPAIR - PPU))
                        first_block["sync"](sp)
                        wait(sp, "sc_ps", n * NHALF)
                        first_block["weights"](sp, 0)
                    if par == 0 and prep:
                        for which in range(2):
                            wait(sp, "prep_sb", 2 * it + which + 1)
                            store_parts(sp, parts_dram, part, bass.ds((it // PPU + 1) * P, P), chunk_at(it % PPU), which, s_[f"out{which}"])
                    if not end:
                        guarded(sp, it + par, lambda: shift_rows(n + 1, 1 - par), {"mx_rows": 6 * 16})
            pairs(sp, pair)
            wait(sp, "sc_ps", B * H * NHALF)
            first_block["weights"](sp, 1)
            store_att(NPAIR - 1)
            wait(sp, "att_out", 16 * NPAIR)

        @block.gpsimd
        def _(pool):
            first_block["gpsimd_start"](pool)
            prime(pool, "dg", "bd_all", "vg", "w", "att_out", "stk0", "stk1", "out0", "out1", "mx_rows")

            def values(m, par):
                nc.gpsimd.tensor_copy(Vg[:, par, :, 0:HD], V_all[:, bass.ds(m, 1)].rearrange("p o k d -> p (o k) d")).then_inc(s_["vg"], 1)

            def weights(half):
                nc.gpsimd.tensor_copy(w_unit[:, :, :, :], w_qk[:, :, :, bass.ds(half * P, P)]).then_inc(s_["w"], 1)

            def bounds(slot):
                wait(pool, "bd", slot + 1)
                nc.gpsimd.tensor_tensor(after_bd, bound[:, 0:1], bound[:, 1:2], ALU.mult)
                nc.gpsimd.partition_all_reduce(bound_all, bound, P, bass.bass_isa.ReduceOp.max).then_inc(s_["bd_all"], 1)

            bounds(0)
            wait(pool, "bd_all", 1)
            nc.gpsimd.memset(Vg, 0.0).then_inc(vg_set, 1)
            pool.wait_ge(vg_set, 1)
            nc.gpsimd.memset(Vg.rearrange("p a k c -> p (a k) c")[:, :, HD:HD + 1], 1.0).then_inc(vg_set, 1)
            pool.wait_ge(vg_set, 2)
            values(0, 0)

            def place_diagonal(n, par, kt):
                if kt == 0:
                    wait(pool, "dexp", n + 1)
                wait(pool, "pv_done", buffer_used(par, n, kt))
                at = slice(kt * P, (kt + 1) * P)
                nc.gpsimd.tensor_tensor(probs[:, probs_of(par, kt), at], diag_s[:, par, at], ones, ALU.mult).then_inc(s_["dg"], 1)

            nc.gpsimd.memset(ones, 1.0).then_inc(vg_set, 1)
            pool.wait_ge(vg_set, 3)

            def pair(it, prep, first, last):
                for par in range(2):
                    n = it * 2 + par
                    for kt in range(KT):
                        place_diagonal(n, par, kt)
                        if kt == 0 and par == 0 and prep:
                            wait(pool, "proj_ps", 2 * it)
                            weights((it // PPU + 1) % KD)
                        if kt == 3 and not (last and par):
                            wait(pool, "pv_done", n * NSTEP)
                            values(n + 1, 1 - par)
                        if kt == KT - 4 and par == 0:
                            bounds(it + 1)
                        if last and par:
                            first_block["gpsimd"](pool, kt)
            pairs(pool, pair)

        @block.vector
        def _(dve):
            first_block["vector_start"](dve)
            prime(dve, *"proj_free prep_link prep_sb o_sb rden_sb att_sb d_sb mx_mul mx_red mx_all mx_neg mx_link mx_part z_add bd bd_link flag".split())

            def prepare(c, which, k, bank):
                at = slice(c * CH, (c + 1) * CH) if isinstance(c, int) else bass.ds(c * CH, CH)
                pt = part[:, which]
                wait(dve, "prep_sb", k)
                wait(dve, "proj_ps", k + 1)
                wait(dve, f"out{which}", k // 2 * 32)
                nc.vector.tensor_tensor(split[:, 0], ps[:, bank], decay[:, which, at], ALU.mult)
                nc.vector.tensor_tensor(split[:, 1], ps[:, bank], decay[:, 1 - which, at], ALU.mult)
                nc.vector.tensor_reduce(bound_new[:, which:which + 1], ps[:, bank], AX.X, ALU.max, apply_absolute_value=True).then_inc(s_["proj_free"], 1)
                wait(dve, "proj_free", k + 1)
                nc.vector.tensor_tensor(bound[:, which:which + 1], bound[:, which:which + 1], bound_new[:, which:which + 1], ALU.max)
                nc.vector.tensor_copy(pt[:, :, 0], split).then_inc(s_["prep_link"], 1)
                wait(dve, "prep_link", 3 * k + 1)
                nc.vector.tensor_tensor(split, split, pt[:, :, 0], ALU.subtract).then_inc(s_["prep_link"], 1)
                wait(dve, "prep_link", 3 * k + 2)
                nc.vector.tensor_copy(pt[:, :, 1], split).then_inc(s_["prep_link"], 1)
                wait(dve, "prep_link", 3 * k + 3)
                nc.vector.tensor_tensor(pt[:, :, 2], split, pt[:, :, 1], ALU.subtract).then_inc(s_["prep_sb"], 1)

            def set_flag(slot):
                wait(dve, "bd_all", slot + 1)
                nc.vector.tensor_tensor(bound_new[:, 0:1], bound_all[:, 0:1], bound_all[:, 1:2], ALU.mult).then_inc(s_["bd_link"], 1)
                wait(dve, "bd_link", slot + 1)
                at = flags[:, slot:slot + 1] if isinstance(slot, int) else flags[:, bass.ds(slot, 1)]
                nc.vector.tensor_scalar(at, bound_new[:, 0:1], SAFE, None, ALU.is_gt).then_inc(s_["flag"], 1)

            def normalise(m, par):
                wait(dve, "pv_done", (m + 1) * NSTEP)
                nc.vector.tensor_copy(O_sb, ps[:, ACC + par]).then_inc(s_["o_sb"], 1)
                wait(dve, "oT_ps", m + 1)
                oT = ps[:, ACC + par].rearrange("p (j c d) -> p j c d", j=CT, c=QC)
                nc.vector.reciprocal(rden, oT[:, :, :, HD]).then_inc(s_["rden_sb"], 1)
                wait(dve, "rden_sb", m + 1)
                if par == 0:
                    wait(dve, "att_out", m // 2 * 16)
                dst = att[:, :, par * HD:(par + 1) * HD].rearrange("p (c j) d -> p j c d", c=QC)
                nc.vector.tensor_tensor(dst, oT[:, :, :, 0:HD], rden.unsqueeze(3).to_broadcast([P, CT, QC, HD]),
                                        ALU.mult).then_inc(s_["att_sb"], 1)

            def diagonals(m, par, bank):
                if not isinstance(m, int) or m > 1:
                    wait(dve, "dg", (m - 1) * KT)
                for c in range(QC):
                    wait(dve, "d_ps", m * QC + c + 1)
                    nc.vector.tensor_tensor(diag_s[:, par, chunk(c)].rearrange("p (j m) -> p j m", m=P),
                                            ps[:, bank].rearrange("p (j m) -> p j m", m=P),
                                            dmask.unsqueeze(1).to_broadcast([P, CT, P]), ALU.mult).then_inc(s_["d_sb"], 1)

            def maxima(m, par, bank):
                for t in range(KT):
                    for kc in range(QC):
                        wait(dve, "mx_ps", m * (KT * QC) + t * QC + kc + 1)
                        if kc == t // CT:
                            blk = ps[:, bank, t % CT * P:(t % CT + 1) * P]
                            nc.vector.tensor_tensor(blk, blk, dmaskT, ALU.mult).then_inc(s_["mx_mul"], 1)
                            wait(dve, "mx_mul", m * KT + t + 1)
                        nc.vector.tensor_reduce(mpart[:, t, kc:kc + 1], ps[:, bank], AX.X, ALU.max).then_inc(s_["mx_red"], 1)
                wait(dve, "mx_red", (m + 1) * (KT * QC))
                nc.vector.tensor_reduce(mneg[:, 0:KT], mpart, AX.X, ALU.max).then_inc(s_["mx_all"], 1)
                wait(dve, "mx_all", m + 1)
                nc.vector.tensor_scalar(mneg[:, 0:KT], mneg[:, 0:KT], -1.0, None, ALU.mult).then_inc(s_["mx_neg"], 1)
                wait(dve, "mxT_ps", m + 1)
                if not isinstance(m, int) or m:
                    wait(dve, "mx_rows", m * (6 * 16))
                nc.vector.tensor_copy(mleft[0:KT], ps[0:KT, bank, 0:P]).then_inc(s_["mx_link"], 1)
                wait(dve, "mx_link", 4 * m + 1)
                nc.vector.tensor_copy(mrow3[0:KT, 0], mleft[0:KT])
                nc.vector.tensor_copy(mrow[0:KT], mleft[0:KT]).then_inc(s_["mx_link"], 1)
                wait(dve, "mx_link", 4 * m + 2)
                nc.vector.tensor_tensor(mleft[0:KT], mrow[0:KT], mrow3[0:KT, 0], ALU.subtract).then_inc(s_["mx_link"], 1)
                wait(dve, "mx_link", 4 * m + 3)
                nc.vector.tensor_copy(mrow3[0:KT, 1], mleft[0:KT]).then_inc(s_["mx_part"], 1)
                wait(dve, "mx_part", m + 1)
                nc.vector.tensor_tensor(mrow3[0:KT, 2], mleft[0:KT], mrow3[0:KT, 1], ALU.subtract).then_inc(s_["mx_link"], 1)
                for c in range(QC):
                    wait(dve, "z_ps", m * QC + c + 1)
                    nc.vector.tensor_tensor(diag_s[:, par, chunk(c)], diag_s[:, par, chunk(c)], ps[:, bank], ALU.add).then_inc(s_["z_add"], 1)

            dve.sem_inc(s_["bd"], 1)
            nc.vector.memset(mneg, 0.0).then_inc(mneg_set, 1)
            dve.wait_ge(mneg_set, 1)
            counts = {"mx_mul": KT, "mx_red": KT * QC, "mx_all": 1, "mx_neg": 1, "mx_link": 4, "mx_part": 1, "z_add": QC}
            diagonals(0, 0, ACC + 1)
            set_flag(0)
            guarded(dve, 0, lambda: maxima(0, 0, ACC + 1), counts)

            def pair(it, prep, first, last):
                for par in range(2):
                    n = it * 2 + par
                    idle = ACC + 1 - par
                    if not (first and par == 0):
                        normalise(n - 1, 1 - par)
                    if par == 0 and prep:
                        for which in range(2):
                            prepare(it % PPU, which, 2 * it + which, idle)
                    if par == 0:
                        wait(dve, "prep_sb", 2 * it + 2 if prep else 2 * (NPAIR - PPU))
                        dve.sem_inc(s_["bd"], 1)
                    else:
                        set_flag(it + 1)
                    if not (last and par):
                        diagonals(n + 1, 1 - par, idle)
                        guarded(dve, it + par, lambda: maxima(n + 1, 1 - par, idle), counts)
            pairs(dve, pair)
            first_block["vector"](dve, 0)
            normalise(B * H - 1, 1)
            first_block["vector"](dve, NSTEP)

        @block.tensor
        def _(pe):
            first_block["tensor_start"](pe)
            prime(pe, *"proj_ps sc_ps pv_done oT_ps d_ps mx_ps mxT_ps z_ps".split())

            def project(at, which, bank):
                for k in range(KD):
                    m = nc.tensor.matmul(ps[:, bank], w_unit[:, which, k], xT[:, k, at:at + CH] if isinstance(at, int) else xT[:, k, bass.ds(at, CH)],
                                         start=k == 0, stop=k == KD - 1)
                m.then_inc(s_["proj_ps"], 1)

            def scores(par, n, s, half):
                wait(pe, "exp_done", halves_read(n, s, half))
                for q0, w, q, k in score_pieces(s, half):
                    m = nc.tensor.matmul(ps[:, half_of(s, half) + q0 // CH % 2, q0 % CH:q0 % CH + w],
                                         stack[0:ROWS + 3, par, k, s * P:(s + 1) * P],
                                         stack[0:ROWS + 3, par, q, q0:q0 + w], start=True, stop=True)
                m.then_inc(s_["sc_ps"], 1)

            def products(par, n, s):
                wait(pe, "dg", n * KT + s + 1)
                wait(pe, "exp_done", n * NHALF + 2 * s + 2)
                for c in range(QC):
                    m = nc.tensor.matmul(ps[STRIP * c:STRIP * (c + 1), ACC + par], Vg[:, par, s], probs[:, probs_of(par, s), chunk(c)],
                                         start=s == 0, stop=s == NSTEP - 1, skip_group_check=True)
                m.then_inc(s_["pv_done"], 1)

            def transposes(m, par):
                wait(pe, "o_sb", m + 1)
                for j in range(CT):
                    i = nc.tensor.transpose(ps[:, ACC + par, j * P:(j + 1) * P], O_sb[:, j * P:(j + 1) * P], ident[:, :])
                i.then_inc(s_["oT_ps"], 1)

            def diagonal(m, par, c, bank):
                for j in range(CT):
                    at = (c * CT + j) * P
                    i = nc.tensor.matmul(ps[:, bank, j * P:(j + 1) * P], stack[0:ROWS, par, KL, at:at + P],
                                         stack[0:ROWS, par, QL, at:at + P], start=True, stop=True)
                i.then_inc(s_["d_ps"], 1)

            def maxima(m, par, bank):
                for t in range(KT):
                    for kc in range(QC):
                        if t or kc:
                            wait(pe, "mx_red", m * (KT * QC) + t * QC + kc)
                        lo, hi = kc * CH, (kc + 1) * CH
                        mid = min(max((t + 1) * P, lo), hi)
                        for a, z, q, k in ((lo, mid, QL, KL), (mid, hi, QU, KU)):
                            if a < z:
                                i = nc.tensor.matmul(ps[:, bank, a - lo:z - lo], stack[0:ROWS, par, q, t * P:(t + 1) * P],
                                                     stack[0:ROWS, par, k, a:z], start=True, stop=True)
                        i.then_inc(s_["mx_ps"], 1)
                wait(pe, "mx_neg", m + 1)
                nc.tensor.transpose(ps[:, bank, 0:P], mneg, ident[:, :]).then_inc(s_["mxT_ps"], 1)
                wait(pe, "mx_link", 4 * m + 1)
                wait(pe, "mx_rows", (m + 1) * (6 * 16))
                for c in range(QC):
                    if c:
                        wait(pe, "z_add", m * QC + c)
                    nc.tensor.matmul(ps[:, bank], stack[ROWS:ROWS + 3, par, KL, 0:P], stack[ROWS:ROWS + 3, par, QL, chunk(c)],
                                     start=True, stop=True).then_inc(s_["z_ps"], 1)

            for c in range(QC):
                if c:
                    wait(pe, "d_sb", c)
                diagonal(0, 0, c, ACC + 1)
            wait(pe, "d_sb", QC)
            counts = {"mx_ps": KT * QC, "mxT_ps": 1, "z_ps": QC}
            guarded(pe, 0, lambda: maxima(0, 0, ACC + 1), counts)

            def pair(it, prep, first, last):
                for par in range(2):
                    n = it * 2 + par
                    idle = ACC + 1 - par
                    end = last and par
                    wait(pe, "vg", n + 1)
                    for s in range(NSTEP):
                        scores(par, n, s, 0)
                        if s >= 2:
                            products(par, n, s - 2)
                        elif not (first and par == 0):
                            products(1 - par, n - 1, NSTEP - 2 + s)
                        scores(par, n, s, 1)
                        if s == 2 and not (first and par == 0):
                            transposes(n - 1, 1 - par)
                        if par == 0 and prep:
                            at = ((it // PPU + 1) // KD) * S + (it % PPU) * CH
                            if s == 4:
                                wait(pe, "w", it + 1)
                                if not first:
                                    wait(pe, "att_sb", n)
                                project(at, 0, idle)
                            if s == 7:
                                wait(pe, "proj_free", 2 * it + 1)
                                project(at, 1, idle)
                        if s >= NSTEP - QC - 1 and s < NSTEP - 1 and not end:
                            c = s - (NSTEP - QC - 1)
                            if c:
                                wait(pe, "d_sb", (n + 1) * QC + c)
                            else:
                                wait(pe, "stk" + str(1 - par), (it + 1) * (16 * STACK_DMAS))
                                if par == 0 and prep:
                                    wait(pe, "proj_free", 2 * it + 2)
                                elif not (first and par == 0):
                                    wait(pe, "att_sb", n)
                            diagonal(n + 1, 1 - par, c, idle)
                        if end:
                            if s == 4:
                                wait(pe, "att_sb", n)
                            first_block["tensor"](pe, s)
                    if not end:
                        wait(pe, "d_sb", (n + 2) * QC)
                        guarded(pe, it + par, lambda: maxima(n + 1, 1 - par, idle), counts)
            pairs(pe, pair)
            for s in (NSTEP - 2, NSTEP - 1):
                products(1, B * H - 1, s)
            first_block["tensor"](pe, NSTEP)
            transposes(B * H - 1, 1)
            first_block["tensor"](pe, NSTEP + 1)

        @block.scalar
        def _(act):
            first_block["scalar_start"](act)
            prime(act, "exp_done", "dexp")

            def pair(it, prep, first, last):
                for par in range(2):
                    n = it * 2 + par
                    wait(act, "d_sb", (n + 1) * QC)
                    wait(act, "z_add", (n + 1) * QC)
                    nc.scalar.activation(diag_s[:, par], diag_s[:, par], ACT.Exp, scale=SCALE).then_inc(s_["dexp"], 1)
                    for s in range(NSTEP):
                        for half in range(2):
                            wait(act, "sc_ps", n * NHALF + 2 * s + half + 1)
                            if half == 0:
                                wait(act, "pv_done", buffer_used(par, n, s))
                            src = ps[:, half_of(s, half):half_of(s, half) + 2].rearrange("p a b -> p (a b)")
                            a, z = half * HALF, (half + 1) * HALF
                            own = s * P
                            parts = [(a, z)] if not a <= own < z else [x for x in ((a, own), (own + P, z)) if x[0] < x[1]]
                            for lo, hi in parts:
                                e = nc.scalar.activation(probs[:, probs_of(par, s), lo:hi], src[:, lo - a:hi - a], ACT.Exp, scale=SCALE)
                            e.then_inc(s_["exp_done"], 1)
                        if last and par:
                            if s == 4:
                                for which in range(2):
                                    wait(act, f"out{which}", (NPAIR // PPU - 1) * (32 * QC))
                            first_block["scalar"](act, s)
            pairs(act, pair)
            first_block["scalar"](act, NSTEP)


def layer(nc, io, sem, ident, xT, V_all, decay, small, w_qk, w_unit, stack, part, work, ps, attn_dram, **rest):
    G, U, DOWN, R, C = 0, 2, 4, 6, 7
    T1, Y, T2, LG, CT_, USES = 0, 2, 4, 6, 7, 8
    NR = HT - NSH
    x1 = V_all[:, :, :, :].rearrange("p h k d -> p h (k d)")
    w_o = w_qk[:, 0]
    combT = decay[0:3 * NE].rearrange("p a t -> p (a t)").bitcast(BF16)[:, 0:T]
    sel = w_unit[0:3 * NE].rearrange("p a k n -> p (a k n)").bitcast(BF16).rearrange("p (h m) -> p h m", m=P)
    big = stack[:, :, :, :].rearrange("p a b s -> p (a b s)").bitcast(F32)
    w_up = big[:, 0:2 * KD * HT * P].rearrange("p (i k h m) -> p i k h m", i=2, k=KD, h=HT)
    w_dn = big[:, 2 * KD * HT * P:2 * KD * HT * P + HT * D].rearrange("p (h d) -> p h d", h=HT)
    hid = carve(work, 0, HT, CH)
    gate = carve(work, 5120, 2, CH)
    zn = carve(work, 6144, CT, D)
    res = carve(work, 7168, 2, CT, D)
    tail = part[:, :, :, :, :].rearrange("p a b i c -> p (a b i c)").bitcast(F32)
    y, xn, x1b = (carve(tail, i * CT * D, CT, D) for i in range(3))
    at_in, x_in = carve(work, 13312, CT, D), carve(work, 14336, CT, D)
    aT, x2s = carve(work, 15360, KD, CH), carve(work, 16384, KD, CH)
    AFTER_ATT = 1088
    bn = [carve(small, AFTER_ATT + 24 * i, CT, 6) for i in range(3)]
    mv = [carve(small, AFTER_ATT + 72 + 8 * i, CT, 2) for i in range(3)]
    var = [carve(small, AFTER_ATT + 96 + 4 * i, CT) for i in range(3)]
    rstd = [carve(small, AFTER_ATT + 108 + 4 * i, CT) for i in range(3)]
    mhalf, neg_mean, shift2 = carve(small, AFTER_ATT + 120, CT), carve(small, AFTER_ATT + 124, CT), carve(small, AFTER_ATT + 128, CT)
    iota = carve(small, AFTER_ATT + 132, NE)
    lmax, zsum, den, wts = carve(small, AFTER_ATT + 148, CT), carve(small, AFTER_ATT + 152, CT), carve(small, AFTER_ATT + 156, CT), carve(small, AFTER_ATT + 160, CT, 2)
    lg, ex, first, comb = (carve(small, AFTER_ATT + 168 + 64 * i, CT, NE) for i in range(4))
    top, idxf = carve(small, AFTER_ATT + 424, CT, 8), carve(small, AFTER_ATT + 456, CT, 8)
    idx = carve(small, AFTER_ATT + 488, CT, 8).bitcast(U32)
    comb3 = carve(small, AFTER_ATT + 520, CT * 3 * NE // 2).bitcast(BF16).rearrange("p (t e) -> p t e", t=CT)
    w_r = carve(small, AFTER_ATT + 616, KD, NE)
    ident_b = carve(small, AFTER_ATT + 648, P // 2).bitcast(BF16)

    names = "r_ps r_cp x1_sb x1_used gate_sb hu_sb h_sb dn_ps z_sb".split()
    s_ = {n: sem("f_" + n) for n in names}
    out_done = [sem(f"out_done{i}") for i in range(2)]
    wait = lambda eng, name, v: eng.wait_ge(s_[name], v + PRIME)
    prime = lambda eng, *ns: [eng.sem_inc(s_[n], PRIME) for n in ns]
    a_in, xr_in, c_in, ffn_in, dn_in = (sem(n) for n in ("a_in", "xr_in", "c_in", "ffn_in", "dn_in"))
    ve1, rs1, ve2, rs2, sh2, ve3, rs3, xn_sb, r_link, lsub_sb, ex_sb, comb_sb, pool_set = (sem("f_" + n) for n in (
        "ve1", "rs1", "ve2", "rs2", "sh2", "ve3", "rs3", "xn_sb", "r_link", "lsub_sb", "ex_sb", "comb_sb", "pool_set"))
    g_ps, u_ps, c_ps, z_link, res_sb = (sem("f_" + n) for n in ("g_ps", "u_ps", "c_ps", "z_link", "res_sb"))
    by_block = lambda ap: ap.rearrange("(n j p) d -> p n j d", j=CT, p=P)
    a_dram = by_block(attn_dram)
    x_dram = by_block(io["L0_attn_x"].rearrange("b s d -> (b s) d"))
    out_dram = by_block(io["out"].rearrange("b s d -> (b s) d"))
    tiles_at = lambda n: slice(n * CT, (n + 1) * CT) if isinstance(n, int) else bass.ds(n * CT, CT)
    block_of = lambda ap, n: ap[:, bass.ds(n, 1)].rearrange("p o j d -> p (o j) d")

    def load(sp, m):
        sp.dma_start(at_in, block_of(a_dram, m)).then_inc(a_in, 16)
        sp.dma_start(x_in, block_of(x_dram, m)).then_inc(xr_in, 16)

    def load_up(sp, i, k):
        r, s = (("L0_ffn_wg_r", "L0_ffn_wg_s"), ("L0_ffn_wu_r", "L0_ffn_wu_s"))[i]
        rows = slice(k * P, (k + 1) * P)
        sp.dma_start(w_up[:, i, k, 0:NSH, :], io[s][:, rows, :].rearrange("e p m -> p e m")).then_inc(ffn_in, 16)
        dst = w_up[:, i, k, NSH:, :].rearrange("p h m -> p (h m)").rearrange("p (e m) -> p e m", e=NE)
        sp.dma_start(dst, io[r][:, rows, :].rearrange("e p m -> p e m")).then_inc(ffn_in, 16)

    def first_factors(pool, r):
        pool.wait_ge(ve1, r + 1)
        nc.gpsimd.tensor_tensor(rstd[0], var[0], mhalf, ALU.pow).then_inc(rs1, 1)

    def second_factors(pool, r):
        pool.wait_ge(ve2, r + 1)
        nc.gpsimd.tensor_tensor(rstd[1], var[1], mhalf, ALU.pow).then_inc(rs2, 1)
        pool.wait_ge(rs2, r + 1)
        nc.gpsimd.tensor_tensor(shift2, neg_mean, rstd[1], ALU.mult).then_inc(sh2, 1)

    def second_norm(act, r):
        act.wait_ge(sh2, r + 1)
        for j in range(CT):
            i_ = nc.scalar.activation(xn[:, j], x1b[:, j], ACT.Identity, bias=shift2[:, j:j + 1], scale=rstd[1][:, j:j + 1])
        i_.then_inc(xn_sb, 1)

    def keep_x1(act, r):
        nc.scalar.copy(x1[:, tiles_at(r), :], x1b).then_inc(s_["x1_used"], 1)

    def copy_out(act, r, use):
        wait(act, "r_ps", r * USES + use + 1)
        if use < Y:
            e = nc.scalar.copy(aT[:, use - T1], ps[:, R])
        elif use < T2:
            if use == Y:
                wait(act, "x1_sb", r)
            h = 2 * (use - Y)
            e = nc.scalar.copy(y[:, h:h + 2], ps[:, R].rearrange("p (j d) -> p j d", j=2))
        elif use < LG:
            nc.scalar.copy(x2s[:, use - T2], ps[:, R])
            e = nc.scalar.copy(xT[:, use - T2, chunk_at(r)], ps[:, R])
        elif use == LG:
            e = nc.scalar.copy(lg, ps[:, R, 0:CT * NE].rearrange("p (j e) -> p j e", j=CT))
        else:
            e = nc.scalar.copy(combT[:, chunk_at(r)], ps[0:3 * NE, R])
        e.then_inc(s_["r_cp"], 1)

    def exps(act, r):
        act.wait_ge(lsub_sb, r + 1)
        nc.scalar.activation(ex, lg, ACT.Exp).then_inc(ex_sb, 1)

    def router(pe, r, use):
        wait(pe, "r_cp", r * USES + use)
        if use == T1:
            pe.wait_ge(a_in, r * 16 + 16)
        if use == T2:
            pe.wait_ge(xn_sb, r + 1)
        if use == CT_:
            pe.wait_ge(comb_sb, r + 1)
        bank = ps[:, R]
        if use < Y:
            for j in range(CT):
                m = nc.tensor.transpose(bank[:, j * P:(j + 1) * P], at_in[:, j, use * P:(use + 1) * P], ident[:, :])
        elif use < T2:
            for j in range(2):
                at = (2 * (use - Y) + j) * P
                for k in range(KD):
                    m = nc.tensor.matmul(bank[:, j * D:(j + 1) * D], aT[:, k, at:at + P], w_o[:, k], start=k == 0, stop=k == KD - 1)
        elif use < LG:
            k = use - T2
            for j in range(CT):
                m = nc.tensor.transpose(bank[:, j * P:(j + 1) * P], xn[:, j, k * P:(k + 1) * P], ident[:, :])
        elif use == LG:
            for j in range(CT):
                for k in range(KD):
                    m = nc.tensor.matmul(bank[:, j * NE:(j + 1) * NE], x2s[:, k, j * P:(j + 1) * P], w_r[:, k],
                                         start=k == 0, stop=k == KD - 1)
        else:
            for j in range(CT):
                m = nc.tensor.matmul(ps[0:3 * NE, R, j * P:(j + 1) * P], comb3[:, j], ident_b, start=True, stop=True)
        m.then_inc(s_["r_ps"], 1)

    LINKS = 16
    count = [0]

    def link(dve, ins, r):
        count[0] += 1
        ins.then_inc(r_link, 1)
        dve.wait_ge(r_link, r * LINKS + count[0])

    def statistics(i, src, link):
        for j in range(CT):
            i_ = nc.vector.bn_stats(bn[i][:, j], src(j))
        link(i_)
        nc.vector.memset(var[i], LN_EPS)
        for j in range(CT):
            i_ = nc.vector.bn_aggr(mv[i][:, j], bn[i][:, j])
        link(i_)

    def first_statistics(dve, r):
        count[0] = 0
        wait(dve, "r_cp", r * USES + T2)
        statistics(0, lambda j: y[:, j], lambda ins: link(dve, ins, r))
        nc.vector.tensor_tensor(var[0], var[0], mv[0][:, :, 1], ALU.add).then_inc(ve1, 1)

    def first_norm(dve, r):
        dve.wait_ge(rs1, r + 1)
        for j in range(CT):
            i_ = nc.vector.tensor_scalar(y[:, j], y[:, j], mv[0][:, j, 0:1], rstd[0][:, j:j + 1], ALU.subtract, ALU.mult)
        link(dve, i_, r)
        dve.wait_ge(xr_in, r * 16 + 16)
        wait(dve, "x1_used", r)
        nc.vector.tensor_tensor(x1b, y, x_in, ALU.add).then_inc(s_["x1_sb"], 1)

    def second_statistics(dve, r):
        wait(dve, "x1_sb", r + 1)
        statistics(1, lambda j: x1b[:, j], lambda ins: link(dve, ins, r))
        nc.vector.tensor_scalar(neg_mean, mv[1][:, :, 0], -1.0, None, ALU.mult)
        nc.vector.tensor_tensor(var[1], var[1], mv[1][:, :, 1], ALU.add).then_inc(ve2, 1)

    def top_two(dve, r):
        bc = lambda v, w: v.unsqueeze(2).to_broadcast([P, CT, w])
        wait(dve, "r_cp", r * USES + CT_)
        link(dve, nc.vector.tensor_reduce(lmax, lg, AX.X, ALU.max), r)
        nc.vector.tensor_tensor(lg, lg, bc(lmax, NE), ALU.subtract).then_inc(lsub_sb, 1)
        dve.wait_ge(ex_sb, r + 1)
        nc.vector.tensor_reduce(zsum, ex, AX.X, ALU.add)
        for j in range(CT):
            i_ = nc.vector.max(top[:, j], ex[:, j])
        link(dve, i_, r)
        nc.vector.scalar_tensor_tensor(den, zsum, TOP_EPS, top[:, :, 0], ALU.mult, ALU.add)
        for j in range(CT):
            i_ = nc.vector.max_index(idx[:, j], top[:, j], ex[:, j])
        link(dve, i_, r)
        nc.vector.tensor_copy(idxf, idx)
        link(dve, nc.vector.tensor_tensor(den, den, top[:, :, 1], ALU.add), r)
        link(dve, nc.vector.reciprocal(den, den), r)
        link(dve, nc.vector.tensor_tensor(wts, top[:, :, 0:2], bc(den, 2), ALU.mult), r)
        for j in range(CT):
            i_ = nc.vector.tensor_scalar(first[:, j], iota, idxf[:, j, 0:1], wts[:, j, 0:1], ALU.is_equal, ALU.mult)
        for j in range(CT):
            i_ = nc.vector.tensor_scalar(comb[:, j], iota, idxf[:, j, 1:2], wts[:, j, 1:2], ALU.is_equal, ALU.mult)
        link(dve, i_, r)
        link(dve, nc.vector.tensor_tensor(comb, comb, first, ALU.add), r)
        for i in range(2):
            at = slice(i * NE, (i + 1) * NE)
            link(dve, nc.vector.tensor_copy(comb3[:, :, at], comb), r)
            if i == 0:
                link(dve, nc.vector.tensor_tensor(comb, comb, comb3[:, :, at], ALU.subtract), r)
        nc.vector.tensor_tensor(comb3[:, :, 2 * NE:], comb, comb3[:, :, at], ALU.subtract).then_inc(comb_sb, 1)
        dve.wait_ge(comb_sb, r + 1)
        assert count[0] == LINKS, count

    def sync_first(sp):
        load(sp, 0)
        sp.dma_start(w_o, io["L0_attn_W_o"].rearrange("(k p) n -> p k n", p=P)).then_inc(c_in, 16)
        sp.dma_start(w_r, io["L0_ffn_router_w"].rearrange("(k p) n -> p k n", p=P)).then_inc(c_in, 16)
        sp.dma_start(iota, io["c_iota"]).then_inc(c_in, 16)
        sp.dma_start(sel.rearrange("p h m -> p (h m)").bitcast(F32), io["c_sel"]).then_inc(c_in, 16)

    def sync_weights(sp, half):
        if half == 0:
            for i, k in ((0, 0), (0, 1), (1, 0)):
                load_up(sp, i, k)
        else:
            load_up(sp, 1, 1)
            sp.dma_start(w_dn[:, 0:NSH], io["L0_ffn_wd_s"].rearrange("e m d -> m e d")).then_inc(dn_in, 16)
            sp.dma_start(w_dn[:, NSH:], io["L0_ffn_wd_r"].rearrange("(h e) m d -> (e m) h d", e=EPT)).then_inc(dn_in, 16)

    def gpsimd_start(pool):
        for par in range(2):
            pool.sem_inc(out_done[par], PRIME)
        nc.gpsimd.memset(mhalf, -0.5).then_inc(pool_set, 1)
        nc.gpsimd.tensor_copy(ident_b, ident[:, :]).then_inc(pool_set, 1)
        pool.wait_ge(pool_set, 2)

    def gpsimd_first(pool, s):
        if s == 10:
            first_factors(pool, 0)
        if s == 12:
            second_factors(pool, 0)

    def vector_start(dve):
        prime(dve, "x1_sb", "hu_sb", "h_sb", "z_sb")

    def vector_first(dve, s):
        if s == KT:
            top_two(dve, 0)
        else:
            dve.wait_ge(c_in, 4 * 16)
            dve.wait_ge(pool_set, 2)
            first_statistics(dve, 0)
            first_norm(dve, 0)
            second_statistics(dve, 0)

    def tensor_start(pe):
        prime(pe, "r_ps", "dn_ps")

    def tensor_first(pe, s):
        if s == 4:
            pe.wait_ge(c_in, 4 * 16)
            pe.wait_ge(pool_set, 2)
        if 4 <= s < 8:
            router(pe, 0, T1 + s - 4)
        if s >= 14:
            router(pe, 0, T2 + s - 14)

    def scalar_start(act):
        prime(act, "r_cp", "x1_used", "gate_sb")

    def scalar_first(act, s):
        if 4 <= s < 8:
            copy_out(act, 0, T1 + s - 4)
        if s == 12:
            second_norm(act, 0)
        if s >= 14:
            copy_out(act, 0, T2 + s - 14)
        if s == KT:
            exps(act, 0)
            keep_x1(act, 0)
            copy_out(act, 0, CT_)

    first_block = dict(sync=sync_first, weights=sync_weights, gpsimd_start=gpsimd_start, gpsimd=gpsimd_first,
                       vector_start=vector_start, vector=vector_first, tensor_start=tensor_start, tensor=tensor_first,
                       scalar_start=scalar_start, scalar=scalar_first)
    attention(nc=nc, io=io, sem=sem, ident=ident, xT=xT, V_all=V_all, decay=decay, small=small, w_qk=w_qk, w_unit=w_unit,
              stack=stack, part=part, work=work, ps=ps, attn_dram=attn_dram, first_block=first_block, **rest)

    def blocks(eng, body):
        with eng.Fori(0, NB // 2 - 1) as i:
            for par in range(2):
                body(i * 2 + par, par, i * 2 + par + 1)
        body(NB - 2, 0, NB - 1)
        body(NB - 1, 1, None)

    with nc.Block() as block:
        @block.sync
        def _(sp):
            load(sp, 1)

            def reload(m):
                wait(sp, "x1_sb", m)
                load(sp, m)

            def store(n, par):
                sp.wait_ge(res_sb, n + 1)
                sp.dma_start(block_of(out_dram, n), res[:, par]).then_inc(out_done[par], 16)

            with sp.Fori(0, NB // 2 - 1) as i:
                for par in range(2):
                    reload(i * 2 + par + 2)
                    store(i * 2 + par, par)
            for n in range(NB - 2, NB):
                store(n, n % 2)
            for par in range(2):
                sp.wait_ge(out_done[par], 16 * NB // 2 + PRIME)

        @block.gpsimd
        def _(pool):
            def body(n, par, r):
                if r is not None:
                    first_factors(pool, r)
                    second_factors(pool, r)
                pool.wait_ge(ve3, n + 1)
                nc.gpsimd.tensor_tensor(rstd[2], var[2], mhalf, ALU.pow).then_inc(rs3, 1)
            blocks(pool, body)

        @block.scalar
        def _(act):
            def body(n, par, r):
                for h in range(HT):
                    act.wait_ge(g_ps, n * HT + h + 1)
                    wait(act, "hu_sb", n * HT + (h - 1 if h >= 2 else 0))
                    nc.scalar.activation(gate[:, h % 2], ps[:, G + h % 2], ACT.Silu).then_inc(s_["gate_sb"], 1)
                    if r is not None:
                        if h < T2:
                            copy_out(act, r, h)
                        if h == HT - 3:
                            second_norm(act, r)
                        if h >= HT - 2:
                            copy_out(act, r, T2 + h - (HT - 2))
                if r is not None:
                    copy_out(act, r, LG)
                    exps(act, r)
                    keep_x1(act, r)
                    copy_out(act, r, CT_)
            blocks(act, body)

        @block.tensor
        def _(pe):
            pe.wait_ge(c_in, 4 * 16)
            pe.wait_ge(ffn_in, 16 * (4 * KD))

            def body(n, par, r):
                x = lambda k: xT[:, k, chunk_at(n)]
                slot = lambda use: router(pe, r, use) if r is not None else None
                wait(pe, "r_cp", n * USES + CT_)
                for h in range(HT):
                    wait(pe, "gate_sb", n * HT + (h - 1 if h >= 2 else 0))
                    for k in range(KD):
                        m = nc.tensor.matmul(ps[:, G + h % 2], w_up[:, 0, k, h], x(k), start=k == 0, stop=k == KD - 1)
                    m.then_inc(g_ps, 1)
                    wait(pe, "hu_sb", n * HT + (h - 1 if h >= 2 else 0))
                    if h == NSH:
                        wait(pe, "r_cp", (n + 1) * USES)
                    if h > NSH:
                        wait(pe, "h_sb", n * NR + h - NSH)
                    for k in range(KD):
                        m = nc.tensor.matmul(ps[:, U + h % 2], w_up[:, 1, k, h], x(k), start=k == 0, stop=k == KD - 1)
                    m.then_inc(u_ps, 1)
                    if h >= NSH:
                        nc.tensor.matmul(ps[:, C], sel[:, h - NSH], combT[:, chunk_at(n)], start=True, stop=True).then_inc(c_ps, 1)
                    if h < T2:
                        slot(h)
                    if h >= HT - 2:
                        slot(T2 + h - (HT - 2))
                pe.wait_ge(dn_in, 2 * 16)
                wait(pe, "z_sb", n)
                wait(pe, "h_sb", (n + 1) * NR - 1)
                for j in range(CT):
                    for h in range(HT):
                        if j == 0 and h == HT - 1:
                            wait(pe, "h_sb", (n + 1) * NR)
                        m = nc.tensor.matmul(ps[:, DOWN + j // 2, (j % 2) * D:(j % 2 + 1) * D], hid[:, h, j * P:(j + 1) * P], w_dn[:, h],
                                             start=h == 0, stop=h == HT - 1)
                    if j == CT - 1:
                        m.then_inc(s_["dn_ps"], 1)
                    if j == 0:
                        slot(LG)
                slot(CT_)
            blocks(pe, body)

        @block.vector
        def _(dve):
            zcount = [0]

            def last_norm(n, par, i):
                def zlink(ins):
                    zcount[0] += 1
                    ins.then_inc(z_link, 1)
                    dve.wait_ge(z_link, n * 2 + zcount[0])

                zcount[0] = 0
                sums = lambda j: ps[:, DOWN + j // 2, (j % 2) * D:(j % 2 + 1) * D]
                wait(dve, "dn_ps", n + 1)
                statistics(2, sums, zlink)
                nc.vector.tensor_tensor(var[2], var[2], mv[2][:, :, 1], ALU.add).then_inc(ve3, 1)
                dve.wait_ge(rs3, n + 1)
                for j in range(CT):
                    i_ = nc.vector.tensor_scalar(zn[:, j], sums(j), mv[2][:, j, 0:1], rstd[2][:, j:j + 1], ALU.subtract, ALU.mult)
                i_.then_inc(s_["z_sb"], 1)
                wait(dve, "z_sb", n + 1)
                wait(dve, "x1_used", n + 1)
                dve.wait_ge(out_done[par], i * 16 + PRIME)
                nc.vector.tensor_tensor(res[:, par], zn, x1[:, tiles_at(n), :], ALU.add).then_inc(res_sb, 1)


            def body(n, par, r):
                for h in range(HT):
                    dve.wait_ge(u_ps, n * HT + h + 1)
                    wait(dve, "gate_sb", n * HT + h + 1)
                    nc.vector.tensor_tensor(hid[:, h], gate[:, h % 2], ps[:, U + h % 2], ALU.mult).then_inc(s_["hu_sb"], 1)
                    if h >= NSH:
                        dve.wait_ge(c_ps, n * NR + h - NSH + 1)
                        wait(dve, "hu_sb", n * HT + h + 1)
                        nc.vector.tensor_tensor(hid[:, h], hid[:, h], ps[:, C], ALU.mult).then_inc(s_["h_sb"], 1)
                    if r is not None:
                        if h == 4:
                            first_statistics(dve, r)
                        if h == 5:
                            first_norm(dve, r)
                        if h == 6:
                            second_statistics(dve, r)
                if r is not None:
                    top_two(dve, r)
                last_norm(n, par, (n - par) // 2)
            blocks(dve, body)


_INS = ["L0_attn_x", "L0_attn_W_q", "L0_attn_W_k", "L0_attn_W_v", "L0_attn_W_o", "L0_attn_W_down_kv", "L0_attn_W_up_k",
        "L0_attn_W_up_v", "L0_ffn_router_w", "L0_ffn_wg_r", "L0_ffn_wu_r", "L0_ffn_wd_r", "L0_ffn_wg_s", "L0_ffn_wu_s",
        "L0_ffn_wd_s"]


def constants():
    t = np.arange(S, dtype=np.float64) - S // 2
    decay = np.exp(np.array([-DECAY, DECAY])[:, None, None] * np.broadcast_to(t, (STRIP, S)))
    s, q = np.arange(P)[:, None], np.arange(P)[None, :]
    diag = np.where(s > q, np.exp(-2 * DECAY * (s - q)), 1.0)
    sel = np.zeros((NE, HT - NSH, P))
    for e in range(NE):
        sel[e, e // EPT, (e % EPT) * MR:(e % EPT + 1) * MR] = 1.0
    out = {"c_ident": np.eye(P), "c_decay": decay, "c_diag": np.stack([diag, diag.T]), "c_sel": np.tile(sel.reshape(NE, -1)[:, ::2], (3, 1)) * BF16_ONES,
           "c_iota": np.tile(np.arange(NE), (P, 1))}
    return {k: np.ascontiguousarray(v, dtype=np.float32) for k, v in out.items()}


def kernel(**inputs):
    import numpy as _np
    import concourse.bacc as _bacc
    from concourse import mybir as _mybir
    from concourse.bass_utils import run_bass_kernel_spmd as _run

    nc = _bacc.Bacc("TRN2", target_bir_lowering=False, num_devices=1)
    arrays, io = {}, {}
    for name, a in [(n, _np.ascontiguousarray(inputs[n])) for n in _INS] + list(constants().items()):
        arrays[f"in_{name}"] = a
        io[name] = nc.dram_tensor(f"in_{name}", a.shape, _mybir.dt.from_np(a.dtype), kind="ExternalInput").ap()
    io["out"] = nc.dram_tensor("out_0", (B, S, D), _mybir.dt.float32, kind="ExternalOutput").ap()
    emit(nc, io)
    r = _run(nc, [arrays], core_ids=[0])
    return r.results[0]["out_0"]
```
